# Optimizing a Trainium2 kernel written in Bass

```python
import numpy as np
import jax
import jax.numpy as jnp

def _softmax(x, axis=-1):
    return jax.nn.softmax(x, axis=axis)

def _gelu(x):
    return jax.nn.gelu(x, approximate=True)

def _silu(x):
    return jax.nn.silu(x)

def _sigmoid(x):
    return jax.nn.sigmoid(x)

def _layernorm(x, axis=-1, eps=1e-05):
    m = jnp.mean(x, axis=axis, keepdims=True)
    v = jnp.var(x, axis=axis, keepdims=True)
    return (x - m) / jnp.sqrt(v + eps)

def _scatter_add(tgt, idx, src, axis=0):
    return tgt.at[idx].add(src)

def _segment_sum(src, seg, n):
    return jax.ops.segment_sum(src, seg, n)
kernel_name = 'mk_audio_tower_d1_tok_audfeat512_r4_3d3e04'

def setup_inputs(seed: int=0):
    np.random.seed(seed)
    _w = jnp.asarray

    def _rec_inputs():
        import jax
        import jax.numpy as jnp
        _rk = jax.random.key(seed)
        x = -0.000124254 + 0.999853 * jax.random.normal(jax.random.fold_in(_rk, 1), (32, 375, 128), jnp.float32)
        return x
    x = _rec_inputs()

    def _L0_tok_setup():
        import jax, jax.numpy as jnp
        import numpy as np
        CONTEXT = (-2, -1, 0, 1, 2)
        EPS = 1e-05
        key = jax.random.key(seed)
        k1, k2 = jax.random.split(key, 2)
        B, T, F = (64, 250, 128)
        O = 128
        C = len(CONTEXT)
        x = jax.random.normal(k1, (B, T, F), dtype=jnp.float32)
        W = jax.random.normal(k2, (O, F * C), dtype=jnp.float32) * 0.02
        b = jnp.zeros((O,), dtype=jnp.float32)
        gamma = jnp.ones((O,), dtype=jnp.float32)
        beta = jnp.zeros((O,), dtype=jnp.float32)
        return {'x': x, 'W': W, 'b': b, 'gamma': gamma, 'beta': beta}
    _L0_tok_all = _L0_tok_setup()
    _L0_tok_in = {k: v for k, v in _L0_tok_all.items() if k in ('W', 'b', 'gamma', 'beta')}
    del _L0_tok_all

    def _L0_attn_setup():
        import jax, jax.numpy as jnp
        import numpy as np
        import math
        D_MODEL = 128
        NUM_HEADS = 8
        HEAD_DIM = D_MODEL // NUM_HEADS
        B, L = (2, 512)
        LN_EPS = 1e-05
        DEN_EPS = 1e-05
        key = jax.random.key(seed)
        ks = jax.random.split(key, 6)
        s = 1.0 / math.sqrt(D_MODEL)
        return {'x': jax.random.normal(ks[0], (B, L, D_MODEL), dtype=jnp.float32), 'Wqkv': jax.random.normal(ks[1], (D_MODEL, 3 * D_MODEL), dtype=jnp.float32) * s, 'bqkv': jnp.zeros((3 * D_MODEL,), dtype=jnp.float32), 'Wout': jax.random.normal(ks[2], (D_MODEL, D_MODEL), dtype=jnp.float32) * s, 'bout': jnp.zeros((D_MODEL,), dtype=jnp.float32), 'ln_gamma': jnp.ones((D_MODEL,), dtype=jnp.float32), 'ln_beta': jnp.zeros((D_MODEL,), dtype=jnp.float32), 'decay_logits': jnp.full((NUM_HEADS,), 5.0, dtype=jnp.float32)}
    _L0_attn_all = _L0_attn_setup()
    _L0_attn_in = {k: v for k, v in _L0_attn_all.items() if k in ('Wqkv', 'bqkv', 'Wout', 'bout', 'ln_gamma', 'ln_beta', 'decay_logits')}
    del _L0_attn_all

    def _L0_ffn_setup():
        import jax, jax.numpy as jnp
        import numpy as np
        B, S, H, E, K, DF, SH = (8, 1024, 128, 8, 2, 128, 128)
        key = jax.random.key(seed)
        ks = jax.random.split(key, 10)
        n = lambda i, shape, sc: jax.random.normal(ks[i], shape, jnp.float32) * sc
        return {'hidden_states': n(0, (B, S, H), 1.0), 'gate_w': n(1, (E, H), 0.05), 'w1': n(2, (E, H, DF), 0.05), 'b1': n(3, (E, DF), 0.01), 'w2': n(4, (E, DF, H), 0.05), 'b2': n(5, (E, H), 0.01), 'sw1': n(6, (H, SH), 0.05), 'sb1': n(7, (SH,), 0.01), 'sw2': n(8, (SH, H), 0.05), 'sb2': n(9, (H,), 0.01)}
    _L0_ffn_all = _L0_ffn_setup()
    _L0_ffn_in = {k: v for k, v in _L0_ffn_all.items() if k in ('gate_w', 'w1', 'b1', 'w2', 'b2', 'sw1', 'sb1', 'sw2', 'sb2')}
    del _L0_ffn_all
    return {'x': x, 'L0_tok_W': _L0_tok_in['W'], 'L0_tok_b': _L0_tok_in['b'], 'L0_tok_gamma': _L0_tok_in['gamma'], 'L0_tok_beta': _L0_tok_in['beta'], 'L0_attn_Wqkv': _L0_attn_in['Wqkv'], 'L0_attn_bqkv': _L0_attn_in['bqkv'], 'L0_attn_Wout': _L0_attn_in['Wout'], 'L0_attn_bout': _L0_attn_in['bout'], 'L0_attn_ln_gamma': _L0_attn_in['ln_gamma'], 'L0_attn_ln_beta': _L0_attn_in['ln_beta'], 'L0_attn_decay_logits': _L0_attn_in['decay_logits'], 'L0_ffn_gate_w': _L0_ffn_in['gate_w'], 'L0_ffn_w1': _L0_ffn_in['w1'], 'L0_ffn_b1': _L0_ffn_in['b1'], 'L0_ffn_w2': _L0_ffn_in['w2'], 'L0_ffn_b2': _L0_ffn_in['b2'], 'L0_ffn_sw1': _L0_ffn_in['sw1'], 'L0_ffn_sb1': _L0_ffn_in['sb1'], 'L0_ffn_sw2': _L0_ffn_in['sw2'], 'L0_ffn_sb2': _L0_ffn_in['sb2']}

def reference(x, L0_tok_W, L0_tok_b, L0_tok_gamma, L0_tok_beta, L0_attn_Wqkv, L0_attn_bqkv, L0_attn_Wout, L0_attn_bout, L0_attn_ln_gamma, L0_attn_ln_beta, L0_attn_decay_logits, L0_ffn_gate_w, L0_ffn_w1, L0_ffn_b1, L0_ffn_w2, L0_ffn_b2, L0_ffn_sw1, L0_ffn_sb1, L0_ffn_sw2, L0_ffn_sb2):
    import jax
    import jax.numpy as jnp

    def _L0_tok_ref(x, W, b, gamma, beta):
        import jax, jax.numpy as jnp
        import numpy as np
        CONTEXT = (-2, -1, 0, 1, 2)
        EPS = 1e-05
        T = x.shape[1]
        width = CONTEXT[-1] - CONTEXT[0]
        T_out = T - width
        xc = jnp.concatenate([x[:, i:i + T_out, :] for i in range(len(CONTEXT))], axis=-1)
        h = jax.nn.relu(jnp.einsum('btf,of->bto', xc, W) + b)
        mean = jnp.mean(h, axis=(0, 1))
        var = jnp.mean(jnp.square(h - mean), axis=(0, 1))
        return gamma * (h - mean) * jax.lax.rsqrt(var + EPS) + beta

    def _L0_attn_ref(x, Wqkv, bqkv, Wout, bout, ln_gamma, ln_beta, decay_logits):
        import jax, jax.numpy as jnp
        import numpy as np
        import math
        D_MODEL = 128
        NUM_HEADS = 8
        HEAD_DIM = D_MODEL // NUM_HEADS
        B, L = (2, 512)
        LN_EPS = 1e-05
        DEN_EPS = 1e-05
        Bv, Lv, D = x.shape
        H = decay_logits.shape[0]
        E = D // H
        qkv = x @ Wqkv + bqkv
        q, k, v = jnp.split(qkv, 3, axis=-1)
        q = q.reshape(Bv, Lv, H, E)
        k = k.reshape(Bv, Lv, H, E)
        v = v.reshape(Bv, Lv, H, E)
        q = (jax.nn.elu(q) + 1.0) / jnp.sqrt(jnp.asarray(E, x.dtype))
        k = jax.nn.elu(k) + 1.0
        lambdas = jax.nn.sigmoid(decay_logits).reshape(1, 1, H, 1)
        t = jnp.arange(Lv, dtype=x.dtype).reshape(1, Lv, 1, 1)
        decay_k = jnp.power(lambdas, -t)
        decay_q = jnp.power(lambdas, t)
        k_dec = k * decay_k
        kv = jnp.einsum('blhe,blhf->blhef', k_dec, v)
        memory = jnp.cumsum(kv, axis=1)
        k_sum = jnp.cumsum(k_dec, axis=1)
        q_dec = q * decay_q
        num = jnp.einsum('blhe,blhef->blhf', q_dec, memory)
        den = jnp.einsum('blhe,blhe->blh', q_dec, k_sum)[..., None] + DEN_EPS
        out = (num / den).reshape(Bv, Lv, D)
        out = out @ Wout + bout
        mu = jnp.mean(out, axis=-1, keepdims=True)
        var = jnp.var(out, axis=-1, keepdims=True)
        out = (out - mu) / jnp.sqrt(var + LN_EPS) * ln_gamma + ln_beta
        return out

    def _L0_ffn_ref(hidden_states, gate_w, w1, b1, w2, b2, sw1, sb1, sw2, sb2):
        import jax, jax.numpy as jnp
        import numpy as np
        B, S, H, E, K, DF, SH = (8, 1024, 128, 8, 2, 128, 128)
        x = hidden_states
        xf = x.reshape(-1, x.shape[-1])
        T = xf.shape[0]
        scores = jax.nn.softmax(xf @ gate_w.T, axis=-1)
        topk_w, topk_i = jax.lax.top_k(scores, K)
        topk_w = topk_w / (topk_w.sum(-1, keepdims=True) + 1e-20)
        combine = jnp.zeros((T, E), xf.dtype).at[jnp.arange(T)[:, None], topk_i].add(topk_w)
        h1 = jax.nn.relu(jnp.einsum('th,ehf->tef', xf, w1) + b1)
        eo = jnp.einsum('tef,efh->teh', h1, w2) + b2
        y = jnp.einsum('te,teh->th', combine, eo)
        shared = jax.nn.relu(xf @ sw1 + sb1) @ sw2 + sb2
        return (y + shared).reshape(x.shape)
    h = _L0_tok_ref(x, L0_tok_W, L0_tok_b, L0_tok_gamma, L0_tok_beta)
    h = h + _L0_attn_ref(_layernorm(h, axis=-1), L0_attn_Wqkv, L0_attn_bqkv, L0_attn_Wout, L0_attn_bout, L0_attn_ln_gamma, L0_attn_ln_beta, L0_attn_decay_logits)
    h = h + _L0_ffn_ref(_layernorm(h, axis=-1), L0_ffn_gate_w, L0_ffn_w1, L0_ffn_b1, L0_ffn_w2, L0_ffn_b2, L0_ffn_sw1, L0_ffn_sb1, L0_ffn_sw2, L0_ffn_sb2)
    return h

_drawn_inputs = setup_inputs


def setup_inputs(seed=0):
    import zlib

    import numpy as np

    out = dict(_drawn_inputs(seed))
    spreads = {'L0_tok_b': (0.0, 0.1),
     'L0_tok_gamma': (1.0, 0.2),
     'L0_tok_beta': (0.0, 0.1),
     'L0_attn_bqkv': (0.0, 0.1),
     'L0_attn_bout': (0.0, 0.1),
     'L0_attn_ln_gamma': (1.0, 0.2),
     'L0_attn_ln_beta': (0.0, 0.1),
     'L0_attn_decay_logits': (5.0, 0.2)}
    factors = {'L0_ffn_b1': 30.193, 'L0_ffn_b2': 8.0, 'L0_ffn_sb1': 8.0, 'L0_ffn_sb2': 7.517}
    for name, (base, spread) in spreads.items():
        noise = np.random.default_rng([zlib.crc32(name.encode()), seed]).standard_normal(out[name].shape)
        drawn = base * np.exp(spread * noise) if base else spread * noise
        out[name] = jnp.asarray(drawn.astype(out[name].dtype))
    for name, factor in factors.items():
        out[name] = (out[name] * factor).astype(out[name].dtype)
    return out
```

```python
from contextlib import ExitStack

import concourse.bass as bass
from concourse import mybir

F32 = mybir.dt.float32
F32R = mybir.dt.float32r
BF16 = mybir.dt.bfloat16
U32 = mybir.dt.uint32
ALU = mybir.AluOpType
ACT = mybir.ActivationFunctionType
AX_X = mybir.AxisListType.X

P = 128
TAPS = 5
HEADS = 8
HD = P // HEADS
PAIRS = HEADS // 2
HALF = HEADS // 2
EXPERTS = 8
UNITS = EXPERTS + 1
PARTS = 3
GATE_COLS = 96
EPS = 1e-5
DEN_EPS = 1e-5


def build(nc, x, tok_w, tok_b, tok_gamma, tok_beta, wqkv, bqkv, wout, bout, ln_gamma, ln_beta,
          decay_logits, gate_w, w1, b1, w2, b2, sw1, sb1, sw2, sb2, out):
    B, T_IN, _ = x.shape
    T = T_IN - (TAPS - 1)
    TILES = -(-T // P)
    TP = TILES * P
    TE = T + T % 2
    XROWS = T_IN // TILES
    XW = TE + TAPS - 1
    LAST = T - (TILES - 1) * P
    assert T_IN == XROWS * TILES and B % 2 == 0 and TP <= 512

    with ExitStack() as ctx:
        def sb(name, shape, dt=F32):
            return ctx.enter_context(nc.sbuf_tensor(name, shape, dt))

        def bank(name):
            return ctx.enter_context(nc.psum_tensor(name, [P, 512], F32))

        def sem(name):
            return ctx.enter_context(nc.semaphore(name))

        ident = sb("ident", [P, P])
        ident_bf = sb("ident_bf", [P, P], BF16)
        causal = sb("causal", [P, P])
        head_block = sb("head_block", [P, P])
        head_mod = sb("head_mod", [P, HALF])
        ones = sb("ones", [P, TP])
        minus_half = sb("minus_half", [P, TILES])
        expert_ids = sb("expert_ids", [P, EXPERTS])
        part_select = sb("part_select", [PARTS * EXPERTS, EXPERTS, P], BF16)
        tok_w_raw = sb("tok_w_raw", [P, TAPS, P])
        gate_raw = sb("gate_raw", [EXPERTS, P])
        gate = sb("gate", [P, GATE_COLS])
        wout_sb = sb("wout_sb", [P, P])
        tok_wf = sb("tok_wf", [P, TAPS, P])
        qkv_raw = sb("qkv_raw", [P, 3, P])
        l1_raw = sb("l1_raw", [P, UNITS, P])
        l2_w = sb("l2_w", [P, UNITS, P])
        tok_hi = sb("tok_hi", [P, TAPS, P], F32R)
        tok_lo = sb("tok_lo", [P, TAPS, P], F32R)
        qkv_hi = sb("qkv_hi", [P, 3, P], F32R)
        qkv_lo = sb("qkv_lo", [P, 3, P], F32R)
        l1_hi = sb("l1_hi", [P, UNITS, P], F32R)
        l1_lo = sb("l1_lo", [P, UNITS, P], F32R)
        b2_raw = sb("b2_raw", [PARTS * EXPERTS, P])
        b2_rest = sb("b2_rest", [PARTS * EXPERTS, 2, P])
        b2_parts = sb("b2_parts", [PARTS * EXPERTS, PARTS, P], BF16)
        l1_bias = sb("l1_bias", [P, UNITS])
        l2_bias = sb("l2_bias", [P, 1])
        tok_vec = sb("tok_vec", [P, 3])
        qkv_bias = sb("qkv_bias", [P, 3])
        qk_bias1 = sb("qk_bias1", [P, 2])
        qk_nbias = sb("qk_nbias", [P, 2])
        den_eps = sb("den_eps", [P, 1])
        eps_sb = sb("eps_sb", [P, TILES])
        fence = sb("fence", [P, 1])
        bout_row = sb("bout_row", [P, P])
        gamma_row = sb("gamma_row", [P, P])
        beta_row = sb("beta_row", [P, P])
        logits_in = sb("logits_in", [P, 1])
        decay = sb("decay", [P, 2, 10])
        powers = sb("powers", [P, 2, 512])

        x_in = sb("x_in", [P, 2, TILES, P])
        x_hi = sb("x_hi", [P, 2, XW], F32R)
        x_lo = sb("x_lo", [P, 2, XW], F32R)
        seqs = sb("seqs", [P, B, TP])
        tok_stats = sb("tok_stats", [P, B, 6])
        tok_mv = sb("tok_mv", [P, 2])
        tok_var = sb("tok_var", [P, 1])
        tok_rstd = sb("tok_rstd", [P, 1])
        bn_scale = sb("bn_scale", [P, 1])
        bn_shift = sb("bn_shift", [P, 1])

        h_fm = sb("h_fm", [P, TP])
        ln_stats = sb("ln_stats", [P, 3, TILES, 6])
        ln_mv = sb("ln_mv", [P, 3, TILES, 2])
        ln_var = sb("ln_var", [P, 3, TILES])
        ln_rstd = sb("ln_rstd", [P, 3, TILES])
        xn_tm = sb("xn_tm", [P, TILES, P])
        xn_hi = sb("xn_hi", [P, TE], F32R)
        xn_lo = sb("xn_lo", [P, TE], F32R)
        q_exp = sb("q_exp", [P, TE])
        k_exp = sb("k_exp", [P, TE])
        q_neg = sb("q_neg", [P, TE])
        k_neg = sb("k_neg", [P, TE])
        q_pos = sb("q_pos", [P, TE])
        k_pos = sb("k_pos", [P, TE])
        q_dec = sb("q_dec", [P, TP])
        k_dec = sb("k_dec", [P, TP])
        q_one = sb("q_one", [P, HALF, TP])
        v_fm = sb("v_fm", [P, TP])
        k_sum = sb("k_sum", [P, TE])
        q_ksum = sb("q_ksum", [P, TE])
        k_tm = sb("k_tm", [P, TILES - 1, P])
        v_par = sb("v_par", [P, TILES * PAIRS, 2, 2 * HD])
        memory = sb("memory", [P, 2, P])
        scores = sb("scores", [P, TILES, HEADS, P])
        den_sb = sb("den_sb", [P, TE])
        rden = sb("rden", [P, TE])
        attn = sb("attn", [P, TP])

        proj = sb("proj", [P, TILES, P])
        proj_n = sb("proj_n", [P, TILES, P])
        proj_g = sb("proj_g", [P, TILES, P])
        x3_tm = sb("x3_tm", [P, TILES, P])
        x3_fm = sb("x3_fm", [P, TP])
        x3_hi = sb("x3_hi", [P, TE], F32R)
        x3_lo = sb("x3_lo", [P, TE], F32R)
        logits = sb("logits", [P, TILES, EXPERTS])
        top8 = sb("top8", [P, TILES, 8])
        top_at = sb("top_at", [P, TILES, 8], U32)
        top_atf = sb("top_atf", [P, TILES, 2])
        is_first = sb("is_first", [P, TILES, EXPERTS])
        is_second = sb("is_second", [P, TILES, EXPERTS])
        chosen = sb("chosen", [P, TILES, EXPERTS])
        shifted = sb("shifted", [P, TILES, EXPERTS])
        expd = sb("expd", [P, TILES, EXPERTS])
        exp_sum = sb("exp_sum", [P, TILES])
        picked = sb("picked", [P, TILES, EXPERTS])
        pick_sum = sb("pick_sum", [P, TILES])
        pick_den = sb("pick_den", [P, TILES])
        pick_rec = sb("pick_rec", [P, TILES])
        combine = sb("combine", [P, TILES, EXPERTS])
        comb_rest = sb("comb_rest", [P, 2, TILES, EXPERTS])
        comb_parts = sb("comb_parts", [P, TILES, PARTS, EXPERTS], BF16)

        comb_fm = sb("comb_fm", [PARTS * EXPERTS, TP], BF16)
        hid = sb("hid", [P, 2, TE])
        mixed = sb("mixed", [P, 2, TE])
        y_fm = sb("y_fm", [P, TP])
        out_sb = sb("out_sb", [P, TILES, P])

        bank_a, bank_b, bank_c, bank_d = bank("bank_a"), bank("bank_b"), bank("bank_c"), bank("bank_d")
        hid_ps = [bank("hid_ps0"), bank("hid_ps1")]
        comb_ps = bank("comb_ps")
        y_ps = bank("y_ps")

        s_const = sem("s_const")
        s_cvec = sem("s_cvec")
        s_tokw = sem("s_tokw")
        s_weights = sem("s_weights")
        s_exp0 = sem("s_exp0")
        s_wt_ps = sem("s_wt_ps")
        s_wt_sb = sem("s_wt_sb")
        s_x = [sem("s_x0"), sem("s_x1")]
        s_xT = sem("s_xT")
        s_xhi = sem("s_xhi")
        s_xlo = sem("s_xlo")
        s_conv = sem("s_conv")
        s_relu = sem("s_relu")
        s_stat = sem("s_stat")
        s_bn = sem("s_bn")
        s_bnp = sem("s_bnp")
        names = ("hfm hT st1 rstd1 xn res xnT xnhi xnlo q k v qneg kneg qexp kexp qpos kpos qdec kdec qone qone2 vfm ksum "
                 "qks kT vT ktm vpar mem_ps mem sc_ps sc num den_ps den rden attn "
                 "proj_ps proj st2 rstd2 projn projg res2 st3 rstd3 x3 x3T x3fm x3hi x3lo gate_ps logits "
                 "route expd combine combT combfm ydone l1 hid cb mix l2 yfm yT outsb store").split()
        S = {n: sem("s_" + n) for n in names}

        block = ctx.enter_context(nc.Block())

        def split3(pe, dst, w_hi, w_lo, m_hi, m_lo, start, stop):
            pe.matmul(dst, w_hi, m_hi, start=start, stop=False)
            pe.matmul(dst, w_lo, m_hi, start=False, stop=False)
            return pe.matmul(dst, w_hi, m_lo, start=False, stop=stop)

        def pairs(eng, body):
            body(0, True, False)
            with eng.Fori(1, B // 2 - 1) as pair:
                body(pair, False, False)
            body(B // 2 - 1, False, True)

        def skewed(eng, step):
            step(-1, True, False, False, False)
            step(0, True, True, False, False)
            step(1, True, True, True, False)
            step(2, True, True, True, True)
            with eng.Fori(3, B - 1) as i:
                step(i, True, True, True, True)
            step(B - 1, False, True, True, True)
            step(B, False, False, True, True)
            step(B + 1, False, False, False, True)

        def diagonal(t, c, n):
            v = t[:, c:c + n]
            return bass.AP(v.tensor, v.offset, [list(v.ap[0]), [4 * HD, n], [3 * HD, 2], [1, HD]])

        def by_tiles(cols):
            return cols.rearrange("p (c n) -> p c n", n=P)

        def over_tiles(row):
            return row.unsqueeze(1).to_broadcast([P, TILES, row.shape[1]])

        def over_cols(cols, n):
            return cols.unsqueeze(2).to_broadcast([P, TILES, n])

        @block.sync
        def _(sp):
            def load_x(b, j):
                sp.dma_start(x_in[0:XROWS, j], x[b].rearrange("(c p) f -> p c f", p=XROWS)).then_inc(s_x[j], 16)

            sp.dma_start(tok_w_raw[:, :, :], tok_w.rearrange("o (i f) -> o i f", i=TAPS)).then_inc(s_tokw, 16)
            load_x(0, 0)
            load_x(1, 1)
            loads = [
                (tok_vec[:, 0:1], tok_b.unsqueeze(1)), (tok_vec[:, 1:2], tok_gamma.unsqueeze(1)),
                (tok_vec[:, 2:3], tok_beta.unsqueeze(1)),
                (logits_in[:, :], bass.AP(decay_logits.tensor, 0, [[1, HEADS], [0, HD], [1, 1]])),
                (gate_raw[:, :], gate_w), (wout_sb[:, :], wout),
                (qkv_raw[:, :, :], wqkv.rearrange("d (j n) -> d j n", j=3)),
                (qkv_bias[:, :], bqkv.rearrange("(j p) -> p j", j=3)),
                (l1_raw[:, 0:EXPERTS], w1.rearrange("e h f -> h e f")), (l1_raw[:, EXPERTS], sw1),
                (l2_w[:, 0:EXPERTS], w2.rearrange("e f h -> f e h")), (l2_w[:, EXPERTS], sw2),
                (l1_bias[:, 0:EXPERTS], b1.rearrange("e f -> f e")), (l1_bias[:, EXPERTS:UNITS], sb1.unsqueeze(1)),
                (l2_bias[:, :], sb2.unsqueeze(1)),
                (bout_row[:, :], bout.partition_broadcast(P)), (gamma_row[:, :], ln_gamma.partition_broadcast(P)),
                (beta_row[:, :], ln_beta.partition_broadcast(P)),
            ] + [(b2_raw[EXPERTS * n:EXPERTS * (n + 1), :], b2) for n in range(PARTS)]
            assert len(loads) == WEIGHT_LOADS
            for dst, src in loads:
                sp.dma_start(dst, src, allow_slow_non_contiguous=True).then_inc(s_weights, 16)
            with sp.Fori(1, B // 2) as pair:
                for j in range(2):
                    sp.wait_ge(s_xT, 2 * pair + j - 1)
                    load_x(2 * pair + j, j)
            with sp.Fori(0, B) as b:
                sp.wait_ge(S["outsb"], b + 1)
                sp.dma_start(out[b, 0:(TILES - 1) * P].rearrange("(c p) f -> p c f", p=P),
                             out_sb[:, 0:TILES - 1]).then_inc(S["store"], 16)
                sp.dma_start(out[b, (TILES - 1) * P:T], out_sb[0:LAST, TILES - 1]).then_inc(S["store"], 16)
            sp.wait_ge(S["store"], 32 * B)

        @block.gpsimd
        def _(pool):
            count = 0

            def made(ins):
                nonlocal count
                count += 1
                ins.then_inc(s_const, 1)

            made(pool.memset(ident[:, :], 0.0))
            made(pool.memset(causal[:, :], 1.0))
            made(pool.memset(head_block[:, :], 1.0))
            made(pool.memset(ones[:, :], 1.0))
            made(pool.memset(minus_half[:, :], -0.5))
            made(pool.memset(part_select[:, :, :], 0.0))
            made(pool.memset(den_eps[:, :], DEN_EPS * HD ** 0.5))
            made(pool.memset(gate[:, :], 0.0))
            made(pool.memset(eps_sb[:, :], EPS))
            for e in range(EXPERTS):
                made(pool.memset(expert_ids[:, e:e + 1], float(e)))
            for t in (h_fm[:, T:TP], q_dec[:, TE:TP], k_dec[:, TE:TP], q_one[:, :, TE:TP], v_fm[:, TE:TP],
                      attn[:, TE:TP], y_fm[:, TE:TP], v_par[:, :, :, :]):
                made(pool.memset(t, 0.0))
            pool.wait_ge(s_const, count)
            made(pool.affine_select(out=ident[:, :], in_=ident[:, :], compare_op=ALU.not_equal, fill=1.0,
                                    base=0, pattern=[[-1, P]], channel_multiplier=1))
            made(pool.affine_select(out=causal[:, :], in_=causal[:, :], compare_op=ALU.is_ge, fill=0.0,
                                    base=0, pattern=[[1, P]], channel_multiplier=-1))
            hb = head_block[:, :].rearrange("p (h e) -> p h e", h=HEADS)
            made(pool.affine_select(out=hb, in_=hb, compare_op=ALU.is_ge, fill=0.0,
                                    base=0, pattern=[[-HD, HEADS], [0, HD]], channel_multiplier=1))
            pool.wait_ge(s_const, count)
            made(pool.affine_select(out=hb, in_=hb, compare_op=ALU.is_ge, fill=0.0,
                                    base=HD - 1, pattern=[[HD, HEADS], [0, HD]], channel_multiplier=-1))
            for part in range(PARTS):
                made(pool.affine_select(out=part_select[:, :, :], in_=part_select[:, :, :],
                                        compare_op=ALU.not_equal, fill=1.0, base=-EXPERTS * part,
                                        pattern=[[-1, EXPERTS], [0, P]], channel_multiplier=1))
                pool.wait_ge(s_const, count)
            assert count == CONSTS

            pool.wait_ge(s_bn, 1)
            pool.tensor_tensor(tok_var[:, :], tok_mv[:, 1:2], eps_sb[:, 0:1], ALU.add).then_inc(s_bnp, 1)
            pool.wait_ge(s_bnp, 1)
            pool.tensor_tensor(tok_rstd[:, :], tok_var[:, :], minus_half[:, 0:1], ALU.pow).then_inc(s_bnp, 1)

            def rstd(n, b, stats, done):
                pool.wait_ge(stats, 2 * TILES * b + 2 * TILES)
                pool.tensor_tensor(ln_var[:, n], ln_mv[:, n, :, 1], eps_sb[:, :], ALU.add).then_inc(done, 1)
                pool.wait_ge(done, 2 * b + 1)
                pool.tensor_tensor(ln_rstd[:, n], ln_var[:, n], minus_half[:, :], ALU.pow).then_inc(done, 1)

            def step(i, s0, s1, s2, s3):
                b = i - 1
                if s1:
                    rstd(0, i, S["st1"], S["rstd1"])
                if s2:
                    rstd(1, b, S["st2"], S["rstd2"])
                    pool.wait_ge(S["projn"], TILES * b + TILES)
                    pool.tensor_tensor(proj_g[:, :, :], proj_n[:, :, :], over_tiles(gamma_row[:, :]), ALU.mult
                                       ).then_inc(S["projg"], 1)
                if s2:
                    pool.wait_ge(S["projg"], b + 1)
                    pool.tensor_tensor(by_tiles(seqs[:, b]), by_tiles(seqs[:, b]), proj_g[:, :, :], ALU.add).then_inc(S["res2"], 1)
                    rstd(2, b, S["st3"], S["rstd3"])
                if s1:
                    pool.wait_ge(S["qdec"], i + 1)
                    pool.wait_ge(S["ksum"], i + 1)
                    pool.tensor_tensor(q_ksum[:, :], q_dec[:, 0:TE], k_sum[:, :], ALU.mult).then_inc(S["qks"], 1)

            skewed(pool, step)

        @block.scalar
        def _(act):
            act.wait_ge(s_weights, 16 * WEIGHT_LOADS)
            act.activation(decay[:, 1, 0:1], logits_in[:, :], ACT.Exp, scale=-1.0).then_inc(s_exp0, 1)

            def x_upper(b, j, first):
                act.wait_ge(s_xT, b + 1)
                if not first:
                    act.wait_ge(s_conv, b - 1)
                act.activation(x_hi[:, j, 0:T_IN], (bank_a, bank_b)[j][:, 0:T_IN], ACT.Copy).then_inc(s_xhi, 1)

            def relu_tok(b, j):
                act.wait_ge(s_conv, b + 1)
                act.activation(seqs[:, b, 0:T], (bank_c, bank_d)[j][:, 0:T], ACT.Relu, bias=tok_vec[:, 0:1]
                               ).then_inc(s_relu, 1)

            def turn(pair, first, last):
                x_upper(2 * pair + 1, 1, first)
                relu_tok(2 * pair, 0)
                if not last:
                    x_upper(2 * pair + 2, 0, False)
                relu_tok(2 * pair + 1, 1)

            x_upper(0, 0, True)
            pairs(act, turn)

            def step(i, s0, s1, s2, s3):
                b2_, b3 = i - 1, i - 2

                def relu(e):
                    if not s3:
                        return
                    act.wait_ge(S["l1"], UNITS * b3 + e + 1)
                    if e < EXPERTS:
                        act.wait_ge(S["mix"], EXPERTS * b3 + max(e - 1, 0))
                        dst = hid[:, e % 2]
                    else:
                        act.wait_ge(S["l2"], UNITS * b3 + e - 1)
                        dst = mixed[:, e % 2]
                    act.activation(dst, hid_ps[e % 2][:, 0:TE], ACT.Relu, bias=l1_bias[:, e:e + 1]
                                   ).then_inc(S["hid"], 1)

                relu(0)
                relu(1)
                if s1:
                    act.wait_ge(S["xnT"], i + 1)
                    act.wait_ge(S["v"], i)
                    act.activation(xn_hi[:, :], bank_c[:, 0:TE], ACT.Copy).then_inc(S["xnhi"], 1)
                relu(2)
                if s1:
                    act.wait_ge(S["q"], i + 1)
                    act.activation(q_neg[:, :], bank_d[:, 0:TE], ACT.Relu, bias=qk_nbias[:, 0:1], scale=-1.0
                                   ).then_inc(S["qneg"], 1)
                    act.wait_ge(S["k"], i + 1)
                    act.activation(k_neg[:, :], bank_a[:, 0:TE], ACT.Relu, bias=qk_nbias[:, 1:2], scale=-1.0
                                   ).then_inc(S["kneg"], 1)
                    act.wait_ge(S["qneg"], i + 1)
                    act.wait_ge(S["qpos"], i)
                    act.activation(q_exp[:, :], q_neg[:, :], ACT.Exp, scale=-1.0).then_inc(S["qexp"], 1)
                    act.wait_ge(S["kneg"], i + 1)
                    act.wait_ge(S["kpos"], i)
                    act.activation(k_exp[:, :], k_neg[:, :], ACT.Exp, scale=-1.0).then_inc(S["kexp"], 1)
                    act.wait_ge(S["v"], i + 1)
                    act.wait_ge(S["vT"], i)
                    act.activation(v_fm[:, 0:TE], bank_b[:, 0:TE], ACT.Identity, bias=qkv_bias[:, 2:3]
                                   ).then_inc(S["vfm"], 1)
                relu(3)
                if s1:
                    act.wait_ge(S["qdec"], i + 1)
                    act.wait_ge(S["sc_ps"], 2 * TILES * i)
                    for m in (0, 1):
                        act.activation(q_one[:, m, 0:TE], q_dec[:, 0:TE], ACT.Copy, scale=head_mod[:, m:m + 1]
                                       ).then_inc(S["qone"], 1)
                relu(4)
                if s1:
                    act.wait_ge(S["kT"], i + 1)
                    act.wait_ge(S["mem_ps"], i)
                    act.activation(k_tm[:, :, :], bank_c[:, 0:(TILES - 1) * P].rearrange("p (c n) -> p c n", n=P),
                                   ACT.Copy).then_inc(S["ktm"], 1)
                    act.wait_ge(S["vT"], i + 1)
                    act.wait_ge(S["num"], TILES * i)
                    act.activation(diagonal(v_par, 0, TILES * PAIRS),
                                   bank_d[:, 0:TP].rearrange("p (g a f) -> p g a f", a=2, f=HD), ACT.Copy
                                   ).then_inc(S["vpar"], 1)
                for e in (5, 6, 7, 8):
                    relu(e)
                if s2:
                    act.wait_ge(S["x3T"], b2_ + 1)
                    act.activation(x3_fm[:, :], bank_b[:, 0:TP], ACT.Copy).then_inc(S["x3fm"], 1)
                    act.activation(x3_hi[:, :], bank_b[:, 0:TE], ACT.Copy).then_inc(S["x3hi"], 1)
                if s1:
                    act.wait_ge(S["den_ps"], i + 1)
                    act.wait_ge(S["rden"], i)
                    act.activation(den_sb[:, :], bank_a[:, 0:TE], ACT.Identity, bias=den_eps[:, 0:1]
                                   ).then_inc(S["den"], 1)
                if s3:
                    act.wait_ge(S["ydone"], b3 + 1)
                    act.wait_ge(S["yT"], b3)
                    act.activation(y_fm[:, 0:TE], y_ps[:, 0:TE], ACT.Identity, bias=l2_bias[:, 0:1]
                                   ).then_inc(S["yfm"], 1)
                if s2:
                    act.wait_ge(S["route"], ROUTE * b2_ + SHIFTED)
                    act.activation(expd[:, :, :], shifted[:, :, :], ACT.Exp).then_inc(S["expd"], 1)

            skewed(act, step)

        @block.tensor
        def _(pe):
            pe.wait_ge(s_const, CONSTS)
            pe.wait_ge(s_tokw, 16)
            for i in range(TAPS):
                dst = bank_c[:, i * P:(i + 1) * P] if i < 4 else bank_d[:, 0:P]
                pe.transpose(dst, tok_w_raw[:, i], ident[:, :]).then_inc(s_wt_ps, 1)

            def transpose_x(pair, j, first):
                pe.wait_ge(s_x[j], 16 * pair + 16)
                if not first:
                    pe.wait_ge(s_xlo, 2 * pair + j - 1)
                for c in range(TILES):
                    ins = pe.transpose((bank_a, bank_b)[j][:, c * XROWS:(c + 1) * XROWS], x_in[0:XROWS, j, c],
                                       ident[0:XROWS, 0:XROWS])
                ins.then_inc(s_xT, 1)

            def conv(pair, j, first):
                b = 2 * pair + j
                pe.wait_ge(s_xlo, b + 1)
                if not first:
                    pe.wait_ge(s_relu, b - 1)
                for i in range(TAPS):
                    ins = split3(pe, (bank_c, bank_d)[j][:, 0:TE], tok_hi[:, i], tok_lo[:, i],
                                 x_hi[:, j, i:i + TE], x_lo[:, j, i:i + TE], i == 0, i == TAPS - 1)
                ins.then_inc(s_conv, 1)

            def turn(pair, first, last):
                transpose_x(pair, 1, first)
                conv(pair, 0, first)
                if not last:
                    transpose_x(pair + 1, 0, False)
                conv(pair, 1, first)

            pe.wait_ge(s_cvec, CVEC_TOK)
            transpose_x(0, 0, True)
            pairs(pe, turn)

            pe.wait_ge(s_weights, 16 * WEIGHT_LOADS)
            pe.wait_ge(s_stat, B)
            pe.transpose(bank_a[:, 0:EXPERTS], gate_raw[:, :], ident[0:EXPERTS, 0:EXPERTS]).then_inc(s_wt_ps, 1)
            pe.wait_ge(s_cvec, CVEC_ALL)

            def tile(t, c):
                return t[:, c * P:(c + 1) * P]

            def step(i, s0, s1, s2, s3):
                b2_, b3 = i - 1, i - 2
                fixed = isinstance(i, int)

                def unit(e):
                    if not s3:
                        return
                    if e < UNITS:
                        pe.wait_ge(S["hid"], UNITS * b3 + max(e - 1, 0))
                        if e == 0:
                            pe.wait_ge(S["x3lo"], b3 + 1)
                        split3(pe, hid_ps[e % 2][:, 0:TE], l1_hi[:, e], l1_lo[:, e], x3_hi[:, :], x3_lo[:, :],
                               True, True).then_inc(S["l1"], 1)
                    if 0 <= e - 1 < EXPERTS:
                        if e == 1:
                            pe.wait_ge(S["combfm"], b3 + 1)
                        pe.wait_ge(S["mix"], EXPERTS * b3 + e - 1)
                        pe.matmul(comb_ps[:, 0:TE], part_select[:, e - 1], comb_fm[:, 0:TE], start=True, stop=True
                                  ).then_inc(S["cb"], 1)
                    f = e - 2
                    if 0 <= f < UNITS:
                        if f == 0:
                            pe.wait_ge(S["yfm"], b3)
                        if f < EXPERTS:
                            pe.wait_ge(S["mix"], EXPERTS * b3 + f + 1)
                        else:
                            pe.wait_ge(S["hid"], UNITS * b3 + UNITS)
                        pe.matmul(y_ps[:, 0:TE], l2_w[:, f], mixed[:, f % 2], start=(f == 0), stop=False
                                  ).then_inc(S["l2"], 1)
                    if f == UNITS - 1:
                        for n in range(PARTS):
                            ins = pe.matmul(y_ps[:, 0:TE], b2_parts[:, n], comb_fm[:, 0:TE], start=False,
                                            stop=(n == PARTS - 1))
                        ins.then_inc(S["ydone"], 1)

                def attend(c):
                    pe.wait_ge(S["sc"], 2 * TILES * i + 2 * c + 2)
                    dst = tile(bank_d, c)
                    if c:
                        pe.matmul(dst, memory[:, c - 1], tile(q_dec, c), start=True, stop=True)
                    for a in range(2):
                        for g in range(PAIRS):
                            rows = slice(2 * HD * g, 2 * HD * (g + 1))
                            ins = pe.matmul(bank_d[rows, c * P:(c + 1) * P], v_par[:, c * PAIRS + g, a],
                                            scores[:, c, 2 * g + a], start=(c == 0 and a == 0),
                                            stop=(c > 0 or a == 1), skip_group_check=(c > 0))
                    ins.then_inc(S["num"], 1)

                def score(c, half, dst):
                    rows = slice(64 * half, 64 * half + 64)
                    pe.matmul(dst[:, :].rearrange("p (m t) -> p m t", m=HALF), k_dec[rows, c * P:(c + 1) * P],
                              q_one[rows, :, c * P:(c + 1) * P], start=True, stop=True).then_inc(S["sc_ps"], 1)

                if s1:
                    pe.wait_ge(S["hfm"], i + 1)
                    pe.wait_ge(S["den"], i)
                    if not fixed or i > 2:
                        pe.wait_ge(S["outsb"], i - 2)
                    for c in range(TILES):
                        ins = pe.transpose(tile(bank_a, c), tile(h_fm, c), ident[:, :])
                    ins.then_inc(S["hT"], 1)
                unit(0)
                if s2:
                    pe.wait_ge(S["attn"], b2_ + 1)
                    pe.wait_ge(S["x3lo"], b2_)
                    for c in range(TILES):
                        ins = pe.matmul(tile(bank_b, c), tile(attn, c), wout_sb[:, :], start=True, stop=True)
                    ins.then_inc(S["proj_ps"], 1)
                if s3:
                    pe.wait_ge(S["combine"], b3 + 1)
                    comb_t = bank_c[:, :].bitcast(BF16)
                    for c in range(TILES):
                        ins = pe.transpose(comb_t[0:PARTS * EXPERTS, c * P:(c + 1) * P],
                                           comb_parts[:, c].rearrange("p n e -> p (n e)"), ident_bf[:, :])
                    ins.then_inc(S["combT"], 1)
                unit(1)
                if s1:
                    pe.wait_ge(S["xn"], TILES * i + TILES)
                    if s3:
                        pe.wait_ge(S["combfm"], b3 + 1)
                    elif i:
                        pe.wait_ge(S["sc"], 2 * TILES * i)
                    for c in range(TILES):
                        ins = pe.transpose(tile(bank_c, c), xn_tm[:, c], ident[:, :])
                    ins.then_inc(S["xnT"], 1)
                unit(2)
                if s1:
                    pe.wait_ge(S["xnlo"], i + 1)
                    pe.wait_ge(S["res"], i + 1)
                    pe.wait_ge(S["attn"], i)
                    for n, (dst, name) in enumerate(((bank_d, "q"), (bank_a, "k"), (bank_b, "v"))):
                        if n == 2 and s2:
                            pe.wait_ge(S["proj"], b2_ + 1)
                        split3(pe, dst[:, 0:TE], qkv_hi[:, n], qkv_lo[:, n], xn_hi[:, :], xn_lo[:, :], True, True
                               ).then_inc(S[name], 1)
                unit(3)
                unit(4)
                if s1:
                    pe.wait_ge(S["kdec"], i + 1)
                    for c in range(TILES - 1):
                        ins = pe.transpose(tile(bank_c, c), tile(k_dec, c), ident[:, :])
                    ins.then_inc(S["kT"], 1)
                    pe.wait_ge(S["vfm"], i + 1)
                    pe.wait_ge(S["qpos"], i + 1)
                    for c in range(TILES):
                        ins = pe.transpose(tile(bank_d, c), tile(v_fm, c), ident[:, :])
                    ins.then_inc(S["vT"], 1)
                unit(5)
                if s1:
                    pe.wait_ge(S["ktm"], i + 1)
                    pe.wait_ge(S["vpar"], i + 1)
                    pe.wait_ge(S["kpos"], i + 1)
                    for n in range(TILES - 1):
                        for c in range(n + 1):
                            ins = pe.matmul(tile(bank_a, n), k_tm[:, c], diagonal(v_par, c * PAIRS, PAIRS),
                                            start=(c == 0), stop=(c == n))
                    ins.then_inc(S["mem_ps"], 1)
                    pe.wait_ge(S["qone"], 2 * i + 2)
                    pe.wait_ge(S["qone2"], 2 * i + 2)
                    score(0, 0, bank_b)
                    score(0, 1, bank_c)
                unit(6)
                if s1:
                    pe.wait_ge(S["mem"], i + 1)
                    score(1, 0, bank_a)
                    pe.wait_ge(S["sc"], 2 * TILES * i + 1)
                    score(1, 1, bank_b)
                    attend(0)
                unit(7)
                if s1:
                    score(2, 0, bank_c)
                    pe.wait_ge(S["sc"], 2 * TILES * i + 3)
                    score(2, 1, bank_a)
                    attend(1)
                unit(8)
                if s2:
                    pe.wait_ge(S["x3"], TILES * b2_ + TILES)
                    if not s1:
                        pe.wait_ge(S["proj"], b2_ + 1)
                    for c in range(TILES):
                        ins = pe.transpose(tile(bank_b, c), x3_tm[:, c], ident[:, :])
                    ins.then_inc(S["x3T"], 1)
                if s1:
                    attend(2)
                    pe.wait_ge(S["qks"], i + 1)
                    pe.matmul(bank_a[:, 0:TE], head_block[:, :], q_ksum[:, :], start=True, stop=True
                              ).then_inc(S["den_ps"], 1)
                unit(9)
                unit(10)
                if s2:
                    pe.wait_ge(S["x3fm"], b2_ + 1)
                    if s3:
                        pe.wait_ge(S["combfm"], b3 + 1)
                    for c in range(TILES):
                        ins = pe.matmul(tile(bank_c, c)[:, 0:GATE_COLS], tile(x3_fm, c), gate[:, :],
                                        start=True, stop=True)
                    ins.then_inc(S["gate_ps"], 1)
                if s3:
                    pe.wait_ge(S["yfm"], b3 + 1)
                    pe.wait_ge(S["den"], i + 1 if s1 else B)
                    for c in range(TILES):
                        ins = pe.transpose(tile(bank_a, c), tile(y_fm, c), ident[:, :])
                    ins.then_inc(S["yT"], 1)

            skewed(pe, step)

        @block.vector
        def _(dve):
            done = 0

            def link(ins):
                nonlocal done
                done += 1
                ins.then_inc(s_cvec, 1)
                dve.wait_ge(s_cvec, done)

            def halves(hi, lo, src):
                link(dve.tensor_copy(hi, src))
                link(dve.tensor_tensor(lo, src, hi.bitcast(F32), ALU.subtract))

            dve.wait_ge(s_const, CONSTS)
            dve.wait_ge(s_wt_ps, TAPS)
            link(dve.tensor_copy(tok_wf[:, 0:4], bank_c[:, :].rearrange("p (i n) -> p i n", n=P)))
            link(dve.tensor_copy(tok_wf[:, 4], bank_d[:, 0:P]))
            halves(tok_hi[:, :, :], tok_lo[:, :, :], tok_wf[:, :, :])
            link(dve.tensor_scalar(x_hi[:, :, T_IN:XW], ones[:, 0:2 * (XW - T_IN)].rearrange(
                "p (a n) -> p a n", a=2), 0.0, None, ALU.mult))
            link(dve.tensor_scalar(x_lo[:, :, T_IN:XW], ones[:, 0:2 * (XW - T_IN)].rearrange(
                "p (a n) -> p a n", a=2), 0.0, None, ALU.mult))
            assert done == CVEC_TOK

            def x_lower(b, j, first):
                dve.wait_ge(s_xhi, b + 1)
                dve.tensor_tensor(x_lo[:, j, 0:T_IN], (bank_a, bank_b)[j][:, 0:T_IN],
                                  x_hi[:, j, 0:T_IN].bitcast(F32), ALU.subtract).then_inc(s_xlo, 1)

            def stats_tok(b):
                dve.wait_ge(s_relu, b + 1)
                dve.bn_stats(tok_stats[:, b], seqs[:, b, 0:T]).then_inc(s_stat, 1)

            def turn(pair, first, last):
                x_lower(2 * pair + 1, 1, first)
                stats_tok(2 * pair)
                if not last:
                    x_lower(2 * pair + 2, 0, False)
                stats_tok(2 * pair + 1)
                if first:
                    prepare()

            def prepare():
                dve.wait_ge(s_weights, 16 * WEIGHT_LOADS)
                halves(qkv_hi[:, :, :], qkv_lo[:, :, :], qkv_raw[:, :, :])
                halves(l1_hi[:, :, :], l1_lo[:, :, :], l1_raw[:, :, :])
                link(dve.tensor_scalar(qk_bias1[:, :], qkv_bias[:, 0:2], 1.0, None, ALU.add))
                link(dve.tensor_scalar(qk_nbias[:, :], qkv_bias[:, 0:2], -1.0, None, ALU.mult))
                link(dve.tensor_copy(ident_bf[:, :], ident[:, :]))
                hm = head_block[:, :].rearrange("p (h e) -> p h e", h=HEADS)
                link(dve.tensor_tensor(head_mod[:, :], hm[:, 0:HALF, 0], hm[:, HALF:HEADS, 0], ALU.add))
                link(dve.tensor_copy(b2_parts[:, 0], b2_raw[:, :]))
                link(dve.tensor_tensor(b2_rest[:, 0], b2_raw[:, :], b2_parts[:, 0], ALU.subtract))
                link(dve.tensor_copy(b2_parts[:, 1], b2_rest[:, 0]))
                link(dve.tensor_tensor(b2_rest[:, 1], b2_rest[:, 0], b2_parts[:, 1], ALU.subtract))
                link(dve.tensor_copy(b2_parts[:, 2], b2_rest[:, 1]))
                dve.wait_ge(s_exp0, 1)
                link(dve.tensor_scalar(decay[:, 1, 0:1], decay[:, 1, 0:1], 1.0, None, ALU.add))
                link(dve.reciprocal(decay[:, 0, 0:1], decay[:, 1, 0:1]))
                link(dve.tensor_copy(powers[:, :, 0:1], ones[:, 0:2].unsqueeze(2)))
                for n in range(9):
                    w = 1 << n
                    for a in range(2):
                        link(dve.tensor_scalar(powers[:, a, w:2 * w], powers[:, a, 0:w], decay[:, a, n:n + 1], None,
                                               ALU.mult))
                    link(dve.tensor_tensor(decay[:, :, n + 1], decay[:, :, n], decay[:, :, n], ALU.mult))

            x_lower(0, 0, True)
            pairs(dve, turn)

            dve.wait_ge(s_wt_ps, TAPS + 1)
            link(dve.tensor_copy(gate[:, 0:EXPERTS], bank_a[:, 0:EXPERTS]))
            dve.wait_ge(s_stat, B)
            dve.bn_aggr(tok_mv[:, :], tok_stats[:, :, :].rearrange("p b s -> p (b s)")).then_inc(s_bn, 1)
            dve.wait_ge(s_bnp, 2)
            link(dve.tensor_tensor(bn_scale[:, :], tok_vec[:, 1:2], tok_rstd[:, :], ALU.mult))
            link(dve.tensor_scalar(bn_shift[:, :], tok_mv[:, 0:1], bn_scale[:, 0:1], tok_vec[:, 2:3],
                                   ALU.mult, ALU.subtract))
            assert done == CVEC_ALL

            def norm_stats(n, b, src, name):
                s = S[name]
                for c in range(TILES):
                    dve.bn_stats(ln_stats[:, n, c], src(c)).then_inc(s, 1)
                for c in range(TILES):
                    if c == 0:
                        dve.wait_ge(s, 2 * TILES * b + TILES)
                        dve.memset(fence[:, :], 0.0)
                    dve.bn_aggr(ln_mv[:, n, c], ln_stats[:, n, c]).then_inc(s, 1)

            def normalize(n, dst, src, name):
                for c in range(TILES):
                    dve.tensor_scalar(dst[:, c], src(c), ln_mv[:, n, c, 0:1], ln_rstd[:, n, c:c + 1],
                                      ALU.subtract, ALU.mult).then_inc(S[name], 1)

            def step(i, s0, s1, s2, s3):
                b2_, b3 = i - 1, i - 2
                fixed = isinstance(i, int)

                def tile_a(c):
                    return bank_a[:, c * P:(c + 1) * P]

                def mix(e):
                    if not s3:
                        return
                    dve.wait_ge(S["hid"], UNITS * b3 + e + 1)
                    dve.wait_ge(S["l2"], UNITS * b3 + max(e - 1, 0))
                    dve.wait_ge(S["cb"], EXPERTS * b3 + e + 1)
                    dve.tensor_tensor(mixed[:, e % 2], hid[:, e % 2], comb_ps[:, 0:TE], ALU.mult
                                      ).then_inc(S["mix"], 1)

                def take_scores(c, n, src):
                    dve.wait_ge(S["sc_ps"], 2 * TILES * i + 2 * c + n + 1)
                    dve.tensor_tensor(scores[:, c, HALF * n:HALF * (n + 1)],
                                      src[:, :].rearrange("p (m t) -> p m t", m=HALF),
                                      causal[:, :].unsqueeze(1).to_broadcast([P, HALF, P]), ALU.mult
                                      ).then_inc(S["sc"], 1)

                if s3:
                    dve.wait_ge(S["ydone"], b3)
                    dve.wait_ge(S["combT"], b3 + 1)
                    dve.tensor_copy(comb_fm[:, :], bank_c[:, :].bitcast(BF16)[0:PARTS * EXPERTS, 0:TP]
                                    ).then_inc(S["combfm"], 1)
                if s1:
                    dve.wait_ge(S["hT"], i + 1)
                    norm_stats(0, i, tile_a, "st1")
                mix(0)
                if s2:
                    dve.wait_ge(S["proj_ps"], b2_ + 1)
                    dve.tensor_tensor(proj[:, :, :], bank_b[:, 0:TP].rearrange("p (c n) -> p c n", n=P),
                                      over_tiles(bout_row[:, :]), ALU.add).then_inc(S["proj"], 1)
                if s1:
                    dve.wait_ge(S["xnT"], i)
                    dve.wait_ge(S["rstd1"], 2 * i + 2)
                    normalize(0, xn_tm, tile_a, "xn")
                    dve.wait_ge(S["hT"], i + 1)
                    dve.tensor_tensor(by_tiles(seqs[:, i]), bank_a[:, 0:TP].rearrange("p (c n) -> p c n", n=P),
                                      over_tiles(beta_row[:, :]), ALU.add).then_inc(S["res"], 1)
                mix(1)
                if s2:
                    dve.wait_ge(S["proj"], b2_ + 1)
                    norm_stats(1, b2_, lambda c: proj[:, c], "st2")
                if s1:
                    dve.wait_ge(S["xnhi"], i + 1)
                    dve.tensor_tensor(xn_lo[:, :], bank_c[:, 0:TE], xn_hi[:, :].bitcast(F32), ALU.subtract
                                      ).then_inc(S["xnlo"], 1)
                if s2:
                    dve.wait_ge(S["rstd2"], 2 * b2_ + 2)
                    dve.wait_ge(S["projg"], b2_)
                    normalize(1, proj_n, lambda c: proj[:, c], "projn")
                mix(2)
                if s1:
                    dve.wait_ge(S["qexp"], i + 1)
                    dve.scalar_tensor_tensor(out=q_pos[:, :], in0=bank_d[:, 0:TE], scalar=qk_bias1[:, 0:1],
                                             in1=q_exp[:, :], op0=ALU.add, op1=ALU.max).then_inc(S["qpos"], 1)
                    dve.wait_ge(S["kexp"], i + 1)
                    dve.scalar_tensor_tensor(out=k_pos[:, :], in0=bank_a[:, 0:TE], scalar=qk_bias1[:, 1:2],
                                             in1=k_exp[:, :], op0=ALU.add, op1=ALU.max).then_inc(S["kpos"], 1)
                    dve.wait_ge(S["qpos"], i + 1)
                    dve.wait_ge(S["num"], TILES * i)
                    dve.wait_ge(S["qks"], i)
                    dve.tensor_tensor(q_dec[:, 0:TE], q_pos[:, :], powers[:, 0, 0:TE], ALU.mult
                                      ).then_inc(S["qdec"], 1)
                    dve.wait_ge(S["kpos"], i + 1)
                    dve.tensor_tensor(k_dec[:, 0:TE], k_pos[:, :], powers[:, 1, 0:TE], ALU.mult
                                      ).then_inc(S["kdec"], 1)
                mix(3)
                if s1:
                    dve.wait_ge(S["qdec"], i + 1)
                    for m in (2, 3):
                        dve.tensor_scalar(q_one[:, m, 0:TE], q_dec[:, 0:TE], head_mod[:, m:m + 1], None, ALU.mult
                                          ).then_inc(S["qone2"], 1)
                    dve.wait_ge(S["kdec"], i + 1)
                    dve.tensor_tensor_scan(k_sum[:, :], ones[:, 0:TE], k_dec[:, 0:TE], 0.0, ALU.mult, ALU.add
                                           ).then_inc(S["ksum"], 1)
                mix(4)
                if s2:
                    dve.wait_ge(S["res2"], b2_ + 1)
                    norm_stats(2, b2_, lambda c: seqs[:, b2_, c * P:(c + 1) * P], "st3")
                if s1:
                    dve.wait_ge(S["mem_ps"], i + 1)
                    dve.wait_ge(S["num"], TILES * i)
                    dve.tensor_tensor(memory[:, :, :], bank_a[:, 0:2 * P].rearrange("p (n m) -> p n m", n=2),
                                      head_block[:, :].unsqueeze(1).to_broadcast([P, 2, P]), ALU.mult
                                      ).then_inc(S["mem"], 1)
                    take_scores(0, 0, bank_b)
                    take_scores(0, 1, bank_c)
                mix(5)
                if s1:
                    take_scores(1, 0, bank_a)
                    take_scores(1, 1, bank_b)
                if s2:
                    dve.wait_ge(S["x3T"], b2_)
                    dve.wait_ge(S["rstd3"], 2 * b2_ + 2)
                    normalize(2, x3_tm, lambda c: seqs[:, b2_, c * P:(c + 1) * P], "x3")
                mix(6)
                if s1:
                    take_scores(2, 0, bank_c)
                    take_scores(2, 1, bank_a)
                mix(7)
                if s2:
                    dve.wait_ge(S["x3hi"], b2_ + 1)
                    dve.tensor_tensor(x3_lo[:, :], bank_b[:, 0:TE], x3_hi[:, :].bitcast(F32), ALU.subtract
                                      ).then_inc(S["x3lo"], 1)
                if s1:
                    dve.wait_ge(S["den"], i + 1)
                    dve.reciprocal(rden[:, :], den_sb[:, :]).then_inc(S["rden"], 1)
                    dve.wait_ge(S["rden"], i + 1)
                    dve.wait_ge(S["proj_ps"], i)
                    dve.wait_ge(S["num"], TILES * i + TILES)
                    dve.tensor_tensor(attn[:, 0:TE], bank_d[:, 0:TE], rden[:, :], ALU.mult).then_inc(S["attn"], 1)
                if s2:
                    route(b2_)
                if s3:
                    dve.wait_ge(S["store"], 32 * b3)
                    dve.wait_ge(S["yT"], b3 + 1)
                    dve.wait_ge(S["yT"], b3 + 1)
                    dve.tensor_tensor(out_sb[:, :, :], bank_a[:, 0:TP].rearrange("p (c n) -> p c n", n=P),
                                      by_tiles(seqs[:, b3]), ALU.add).then_inc(S["outsb"], 1)
                if s0:
                    dve.wait_ge(S["hT"], i + 1 if not fixed or i >= 0 else 0)
                    dve.tensor_scalar(h_fm[:, 0:T], seqs[:, i + 1, 0:T], bn_scale[:, 0:1], bn_shift[:, 0:1],
                                      ALU.mult, ALU.subtract).then_inc(S["hfm"], 1)

            def route(b):
                n = 0

                def then(ins, wait=True):
                    nonlocal n
                    n += 1
                    ins.then_inc(S["route"], 1)
                    if wait:
                        dve.wait_ge(S["route"], ROUTE * b + n)

                gate_out = bank_c[:, 0:TP].rearrange("p (c n) -> p c n", n=P)[:, :, 0:EXPERTS]
                dve.wait_ge(S["gate_ps"], b + 1)
                then(dve.tensor_copy(logits[:, :, :], gate_out), wait=False)
                for c in range(TILES):
                    then(dve.max(top8[:, c], gate_out[:, c]), wait=(c == TILES - 1))
                dve.wait_ge(S["expd"], b)
                then(dve.tensor_tensor(shifted[:, :, :], logits[:, :, :], over_cols(top8[:, :, 0], EXPERTS),
                                       ALU.subtract), wait=False)
                assert n == SHIFTED
                for c in range(TILES):
                    then(dve.max_index(top_at[:, c], top8[:, c], gate_out[:, c]), wait=(c == TILES - 1))
                then(dve.tensor_copy(top_atf[:, :, :], top_at[:, :, 0:2]))
                then(dve.tensor_tensor(is_first[:, :, :], over_tiles(expert_ids[:, :]),
                                       over_cols(top_atf[:, :, 0], EXPERTS), ALU.is_equal), wait=False)
                then(dve.tensor_tensor(is_second[:, :, :], over_tiles(expert_ids[:, :]),
                                       over_cols(top_atf[:, :, 1], EXPERTS), ALU.is_equal))
                then(dve.tensor_tensor(chosen[:, :, :], is_first[:, :, :], is_second[:, :, :], ALU.add))
                dve.wait_ge(S["expd"], b + 1)
                then(dve.tensor_tensor(picked[:, :, :], expd[:, :, :], chosen[:, :, :], ALU.mult), wait=False)
                then(dve.tensor_reduce(exp_sum[:, :], expd[:, :, :], AX_X, ALU.add))
                then(dve.tensor_reduce(pick_sum[:, :], picked[:, :, :], AX_X, ALU.add))
                then(dve.scalar_tensor_tensor(out=pick_den[:, :], in0=exp_sum[:, :], scalar=1e-20,
                                              in1=pick_sum[:, :], op0=ALU.mult, op1=ALU.add))
                then(dve.reciprocal(pick_rec[:, :], pick_den[:, :]))
                then(dve.tensor_tensor(combine[:, :, :], picked[:, :, :], over_cols(pick_rec[:, :], EXPERTS), ALU.mult))
                dve.wait_ge(S["combT"], b)
                then(dve.tensor_copy(comb_parts[:, :, 0], combine[:, :, :]))
                then(dve.tensor_tensor(comb_rest[:, 0], combine[:, :, :], comb_parts[:, :, 0], ALU.subtract))
                then(dve.tensor_copy(comb_parts[:, :, 1], comb_rest[:, 0]))
                then(dve.tensor_tensor(comb_rest[:, 1], comb_rest[:, 0], comb_parts[:, :, 1], ALU.subtract))
                assert n == ROUTE
                dve.tensor_copy(comb_parts[:, :, 2], comb_rest[:, 1]).then_inc(S["combine"], 1)

            skewed(dve, step)


CONSTS = 17 + 8 + 4 + PARTS
WEIGHT_LOADS = 18 + PARTS
CVEC_TOK = 6
CVEC_ALL = 6 + 4 + 4 + 5 + 3 + 27 + 1 + 2
SHIFTED = 5
ROUTE = 22

_INS = ["x", "L0_tok_W", "L0_tok_b", "L0_tok_gamma", "L0_tok_beta", "L0_attn_Wqkv", "L0_attn_bqkv",
        "L0_attn_Wout", "L0_attn_bout", "L0_attn_ln_gamma", "L0_attn_ln_beta", "L0_attn_decay_logits",
        "L0_ffn_gate_w", "L0_ffn_w1", "L0_ffn_b1", "L0_ffn_w2", "L0_ffn_b2", "L0_ffn_sw1", "L0_ffn_sb1",
        "L0_ffn_sw2", "L0_ffn_sb2"]


def kernel(**inputs):
    import numpy as np
    import concourse.bacc as bacc
    from concourse.bass_utils import run_bass_kernel_spmd

    nc = bacc.Bacc("TRN2", target_bir_lowering=False, num_devices=1)
    arrays, args = {}, []
    for name in _INS:
        a = np.ascontiguousarray(inputs[name])
        arrays[f"in_{name}"] = a
        args.append(nc.dram_tensor(f"in_{name}", a.shape, mybir.dt.from_np(a.dtype), kind="ExternalInput").ap())
    b, t, d = inputs["x"].shape
    args.append(nc.dram_tensor("out", (b, t - (TAPS - 1), d), F32, kind="ExternalOutput").ap())
    build(nc, *args)
    r = run_bass_kernel_spmd(nc, [arrays], core_ids=[0])
    return r.results[0]["out"]
```

```python
from contextlib import ExitStack

import concourse.bass as bass
from concourse import mybir

F32 = mybir.dt.float32
F32R = mybir.dt.float32r
BF16 = mybir.dt.bfloat16
U32 = mybir.dt.uint32
ALU = mybir.AluOpType
ACT = mybir.ActivationFunctionType
AX_X = mybir.AxisListType.X

P = 128
TAPS = 5
HEADS = 8
HD = P // HEADS
PAIRS = HEADS // 2
HALF = HEADS // 2
EXPERTS = 8
UNITS = EXPERTS + 1
PARTS = 3
GATE_COLS = 96
EPS = 1e-5
DEN_EPS = 1e-5


def build(nc, x, tok_w, tok_b, tok_gamma, tok_beta, wqkv, bqkv, wout, bout, ln_gamma, ln_beta,
          decay_logits, gate_w, w1, b1, w2, b2, sw1, sb1, sw2, sb2, out):
    B, T_IN, _ = x.shape
    T = T_IN - (TAPS - 1)
    TILES = -(-T // P)
    TP = TILES * P
    TE = T + T % 2
    XROWS = T_IN // TILES
    XW = TE + TAPS - 1
    LAST = T - (TILES - 1) * P
    assert T_IN == XROWS * TILES and B % 2 == 0 and TP <= 512

    with ExitStack() as ctx:
        def sb(name, shape, dt=F32):
            return ctx.enter_context(nc.sbuf_tensor(name, shape, dt))

        def bank(name):
            return ctx.enter_context(nc.psum_tensor(name, [P, 512], F32))

        def sem(name):
            return ctx.enter_context(nc.semaphore(name))

        ident = sb("ident", [P, P])
        ident_bf = sb("ident_bf", [P, P], BF16)
        causal = sb("causal", [P, P])
        head_block = sb("head_block", [P, P])
        head_mod = sb("head_mod", [P, HALF])
        ones = sb("ones", [P, TP])
        minus_half = sb("minus_half", [P, TILES])
        expert_ids = sb("expert_ids", [P, EXPERTS])
        part_select = sb("part_select", [PARTS * EXPERTS, EXPERTS, P], BF16)
        tok_w_raw = sb("tok_w_raw", [P, TAPS, P])
        gate_raw = sb("gate_raw", [EXPERTS, P])
        gate = sb("gate", [P, GATE_COLS])
        wout_sb = sb("wout_sb", [P, P])
        tok_wf = sb("tok_wf", [P, TAPS, P])
        qkv_raw = sb("qkv_raw", [P, 3, P])
        l1_raw = sb("l1_raw", [P, UNITS, P])
        l2_w = sb("l2_w", [P, UNITS, P])
        tok_hi = sb("tok_hi", [P, TAPS, P], F32R)
        tok_lo = sb("tok_lo", [P, TAPS, P], F32R)
        qkv_hi = sb("qkv_hi", [P, 3, P], F32R)
        qkv_lo = sb("qkv_lo", [P, 3, P], F32R)
        l1_hi = sb("l1_hi", [P, UNITS, P], F32R)
        l1_lo = sb("l1_lo", [P, UNITS, P], F32R)
        b2_raw = sb("b2_raw", [PARTS * EXPERTS, P])
        b2_rest = sb("b2_rest", [PARTS * EXPERTS, 2, P])
        b2_parts = sb("b2_parts", [PARTS * EXPERTS, PARTS, P], BF16)
        l1_bias = sb("l1_bias", [P, UNITS])
        l2_bias = sb("l2_bias", [P, 1])
        tok_vec = sb("tok_vec", [P, 3])
        qkv_bias = sb("qkv_bias", [P, 3])
        qk_bias1 = sb("qk_bias1", [P, 2])
        qk_nbias = sb("qk_nbias", [P, 2])
        head_sum = sb("head_sum", [P, GATE_COLS])
        tiny = sb("tiny", [P, TILES])
        zeros = sb("zeros", [P, TILES])
        eps_sb = sb("eps_sb", [P, TILES])
        fence = sb("fence", [P, 1])
        bout_row = sb("bout_row", [P, P])
        gamma_row = sb("gamma_row", [P, P])
        beta_row = sb("beta_row", [P, P])
        logits_in = sb("logits_in", [P, 1])
        decay = sb("decay", [P, 2, 10])
        powers = sb("powers", [P, 2, 512])

        x_in = sb("x_in", [P, 2, TILES, P])
        x_hi = sb("x_hi", [P, 2, XW], F32R)
        x_lo = sb("x_lo", [P, 2, XW], F32R)
        seqs = sb("seqs", [P, B, TP])
        tok_stats = sb("tok_stats", [P, B, 6])
        tok_mv = sb("tok_mv", [P, 2])
        tok_var = sb("tok_var", [P, 1])
        tok_rstd = sb("tok_rstd", [P, 1])
        bn_scale = sb("bn_scale", [P, 1])
        bn_shift = sb("bn_shift", [P, 1])

        h_fm = sb("h_fm", [P, TP])
        ln_stats = sb("ln_stats", [P, 3, TILES, 6])
        ln_mv = sb("ln_mv", [P, 3, TILES, 2])
        ln_var = sb("ln_var", [P, 3, TILES])
        ln_rstd = sb("ln_rstd", [P, 3, TILES])
        ln_nmean = sb("ln_nmean", [P, 3, TILES])
        ln_shift = sb("ln_shift", [P, 3, TILES])
        xn_tm = sb("xn_tm", [P, TILES, P])
        xn_hi = sb("xn_hi", [P, TE], F32R)
        xn_lo = sb("xn_lo", [P, TE], F32R)
        q_exp = sb("q_exp", [P, TE])
        k_exp = sb("k_exp", [P, TE])
        q_neg = sb("q_neg", [P, TE])
        k_neg = sb("k_neg", [P, TE])
        q_pos = sb("q_pos", [P, TE])
        k_pos = sb("k_pos", [P, TE])
        q_dec = sb("q_dec", [P, TP])
        k_dec = sb("k_dec", [P, TP])
        q_one = sb("q_one", [P, HALF, TP])
        v_fm = sb("v_fm", [P, TP])
        k_sum = sb("k_sum", [P, TE])
        q_ksum = sb("q_ksum", [P, TP])
        k_tm = sb("k_tm", [P, TILES - 1, P])
        v_par = sb("v_par", [P, TILES * PAIRS, 2, 2 * HD])
        memory = sb("memory", [P, 2, P])
        scores = sb("scores", [P, TILES, HEADS, P])
        num_sb = sb("num_sb", [P, TP])
        den_tm = sb("den_tm", [P, TILES, HEADS])
        rden = sb("rden", [P, TILES, HEADS])
        attn_tm = sb("attn_tm", [P, TILES, P])
        attn = sb("attn", [P, TP])

        proj = sb("proj", [P, TILES, P])
        proj_n = sb("proj_n", [P, TILES, P])
        proj_g = sb("proj_g", [P, TILES, P])
        x3_tm = sb("x3_tm", [P, TILES, P])
        x3_fm = sb("x3_fm", [P, TP])
        x3_hi = sb("x3_hi", [P, TE], F32R)
        x3_lo = sb("x3_lo", [P, TE], F32R)
        top8 = sb("top8", [P, TILES, 8])
        top_at = sb("top_at", [P, TILES, 8], U32)
        is_top = sb("is_top", [P, TILES, 2, EXPERTS])
        shifted = sb("shifted", [P, TILES, EXPERTS])
        expd = sb("expd", [P, TILES, EXPERTS])
        exp_sum = sb("exp_sum", [P, TILES])
        exp_tiny = sb("exp_tiny", [P, TILES])
        pick_sum = sb("pick_sum", [P, TILES])
        pick_den = sb("pick_den", [P, TILES])
        pick_rec = sb("pick_rec", [P, TILES])
        top_w = sb("top_w", [P, TILES, 2])
        placed = sb("placed", [P, TILES, 2, EXPERTS])
        combine = sb("combine", [P, TILES, EXPERTS])
        comb_rest = sb("comb_rest", [P, TILES, EXPERTS])
        comb_parts = sb("comb_parts", [P, TILES, PARTS, EXPERTS], BF16)

        comb_fm = sb("comb_fm", [PARTS * EXPERTS, TP], BF16)
        hid = sb("hid", [P, 3, TE])
        mixed = sb("mixed", [P, 2, TE])
        y_fm = sb("y_fm", [P, TP])
        out_sb = sb("out_sb", [P, TILES, P])

        bank_a, bank_b, bank_c, bank_d = bank("bank_a"), bank("bank_b"), bank("bank_c"), bank("bank_d")
        hid_ps = [bank("hid_ps0"), bank("hid_ps1")]
        comb_ps = bank("comb_ps")
        y_ps = bank("y_ps")

        s_const = sem("s_const")
        s_cvec = sem("s_cvec")
        s_tokw = sem("s_tokw")
        s_weights = sem("s_weights")
        s_exp0 = sem("s_exp0")
        s_wt_ps = sem("s_wt_ps")
        s_wt_sb = sem("s_wt_sb")
        s_x = [sem("s_x0"), sem("s_x1")]
        s_xT = sem("s_xT")
        s_xhi = sem("s_xhi")
        s_xlo = sem("s_xlo")
        s_conv = sem("s_conv")
        s_relu = sem("s_relu")
        s_stat = sem("s_stat")
        s_bn = sem("s_bn")
        s_bnp = sem("s_bnp")
        names = ("hfm hT st1 rstd1 xn res xnT xnhi xnlo q k v qneg kneg qexp kexp qpos kpos qdec kdec qone qone2 vfm ksum "
                 "qks kT vT ktm vpar mem_ps mem sc_ps sc num numsb den_ps den rden numT attntm attnT attn "
                 "proj_ps proj st2 rstd2 projn projg res2 st3 rstd3 x3 x3T x3fm x3hi x3lo gate_ps top topat istop "
                 "shifted expd expsum pickden pickrec route combine combT combfm ydone l1 hid cb mix l2 yfm yT "
                 "outsb store").split()
        S = {n: sem("s_" + n) for n in names}

        block = ctx.enter_context(nc.Block())

        def split3(pe, dst, w_hi, w_lo, m_hi, m_lo, start, stop):
            pe.matmul(dst, w_hi, m_hi, start=start, stop=False)
            pe.matmul(dst, w_lo, m_hi, start=False, stop=False)
            return pe.matmul(dst, w_hi, m_lo, start=False, stop=stop)

        def pairs(eng, body):
            body(0, True, False)
            with eng.Fori(1, B // 2 - 1) as pair:
                body(pair, False, False)
            body(B // 2 - 1, False, True)

        def skewed(eng, step):
            step(-1, True, False, False, False)
            step(0, True, True, False, False)
            step(1, True, True, True, False)
            step(2, True, True, True, True)
            with eng.Fori(3, B - 1) as i:
                step(i, True, True, True, True)
            step(B - 1, False, True, True, True)
            step(B, False, False, True, True)
            step(B + 1, False, False, False, True)

        def diagonal(t, c, n):
            v = t[:, c:c + n]
            return bass.AP(v.tensor, v.offset, [list(v.ap[0]), [4 * HD, n], [3 * HD, 2], [1, HD]])

        def by_tiles(cols):
            return cols.rearrange("p (c n) -> p c n", n=P)

        def over_tiles(row):
            return row.unsqueeze(1).to_broadcast([P, TILES, row.shape[1]])

        def over_cols(cols, n):
            return cols.unsqueeze(2).to_broadcast([P, TILES, n])

        @block.sync
        def _(sp):
            def load_x(b, j):
                sp.dma_start(x_in[0:XROWS, j], x[b].rearrange("(c p) f -> p c f", p=XROWS)).then_inc(s_x[j], 16)

            sp.dma_start(tok_w_raw[:, :, :], tok_w.rearrange("o (i f) -> o i f", i=TAPS)).then_inc(s_tokw, 16)
            load_x(0, 0)
            load_x(1, 1)
            loads = [
                (tok_vec[:, 0:1], tok_b.unsqueeze(1)), (tok_vec[:, 1:2], tok_gamma.unsqueeze(1)),
                (tok_vec[:, 2:3], tok_beta.unsqueeze(1)),
                (logits_in[:, :], bass.AP(decay_logits.tensor, 0, [[1, HEADS], [0, HD], [1, 1]])),
                (gate_raw[:, :], gate_w), (wout_sb[:, :], wout),
                (qkv_raw[:, :, :], wqkv.rearrange("d (j n) -> d j n", j=3)),
                (qkv_bias[:, :], bqkv.rearrange("(j p) -> p j", j=3)),
                (l1_raw[:, 0:EXPERTS], w1.rearrange("e h f -> h e f")), (l1_raw[:, EXPERTS], sw1),
                (l2_w[:, 0:EXPERTS], w2.rearrange("e f h -> f e h")), (l2_w[:, EXPERTS], sw2),
                (l1_bias[:, 0:EXPERTS], b1.rearrange("e f -> f e")), (l1_bias[:, EXPERTS:UNITS], sb1.unsqueeze(1)),
                (l2_bias[:, :], sb2.unsqueeze(1)),
                (bout_row[:, :], bout.partition_broadcast(P)), (gamma_row[:, :], ln_gamma.partition_broadcast(P)),
                (beta_row[:, :], ln_beta.partition_broadcast(P)),
            ] + [(b2_raw[EXPERTS * n:EXPERTS * (n + 1), :], b2) for n in range(PARTS)]
            assert len(loads) == WEIGHT_LOADS
            for dst, src in loads:
                sp.dma_start(dst, src, allow_slow_non_contiguous=True).then_inc(s_weights, 16)
            with sp.Fori(1, B // 2) as pair:
                for j in range(2):
                    sp.wait_ge(s_xT, 2 * pair + j - 1)
                    load_x(2 * pair + j, j)
            with sp.Fori(0, B) as b:
                sp.wait_ge(S["outsb"], b + 1)
                sp.dma_start(out[b, 0:(TILES - 1) * P].rearrange("(c p) f -> p c f", p=P),
                             out_sb[:, 0:TILES - 1]).then_inc(S["store"], 16)
                sp.dma_start(out[b, (TILES - 1) * P:T], out_sb[0:LAST, TILES - 1]).then_inc(S["store"], 16)
            sp.wait_ge(S["store"], 32 * B)

        @block.gpsimd
        def _(pool):
            count = 0

            def made(ins):
                nonlocal count
                count += 1
                ins.then_inc(s_const, 1)

            made(pool.memset(ident[:, :], 0.0))
            made(pool.memset(causal[:, :], 1.0))
            made(pool.memset(head_block[:, :], 1.0))
            made(pool.memset(ones[:, :], 1.0))
            made(pool.memset(minus_half[:, :], -0.5))
            made(pool.memset(part_select[:, :, :], 0.0))
            made(pool.memset(head_sum[:, :], 0.0))
            made(pool.memset(tiny[:, :], 1e-20))
            made(pool.memset(zeros[:, :], 0.0))
            made(pool.memset(gate[:, :], 0.0))
            made(pool.memset(eps_sb[:, :], EPS))
            for e in range(EXPERTS):
                made(pool.memset(expert_ids[:, e:e + 1], float(e)))
            for t in (h_fm[:, T:TP], q_dec[:, TE:TP], k_dec[:, TE:TP], q_one[:, :, TE:TP], v_fm[:, TE:TP],
                      q_ksum[:, TE:TP], y_fm[:, TE:TP], v_par[:, :, :, :]):
                made(pool.memset(t, 0.0))
            pool.wait_ge(s_const, count)
            made(pool.affine_select(out=ident[:, :], in_=ident[:, :], compare_op=ALU.not_equal, fill=1.0,
                                    base=0, pattern=[[-1, P]], channel_multiplier=1))
            made(pool.affine_select(out=causal[:, :], in_=causal[:, :], compare_op=ALU.is_ge, fill=0.0,
                                    base=0, pattern=[[1, P]], channel_multiplier=-1))
            hb = head_block[:, :].rearrange("p (h e) -> p h e", h=HEADS)
            made(pool.affine_select(out=hb, in_=hb, compare_op=ALU.is_ge, fill=0.0,
                                    base=0, pattern=[[-HD, HEADS], [0, HD]], channel_multiplier=1))
            pool.wait_ge(s_const, count)
            made(pool.affine_select(out=hb, in_=hb, compare_op=ALU.is_ge, fill=0.0,
                                    base=HD - 1, pattern=[[HD, HEADS], [0, HD]], channel_multiplier=-1))
            for part in range(PARTS):
                made(pool.affine_select(out=part_select[:, :, :], in_=part_select[:, :, :],
                                        compare_op=ALU.not_equal, fill=1.0, base=-EXPERTS * part,
                                        pattern=[[-1, EXPERTS], [0, P]], channel_multiplier=1))
                pool.wait_ge(s_const, count)
            assert count == CONSTS

            pool.wait_ge(s_bn, 1)
            pool.tensor_tensor(tok_var[:, :], tok_mv[:, 1:2], eps_sb[:, 0:1], ALU.add).then_inc(s_bnp, 1)
            pool.wait_ge(s_bnp, 1)
            pool.tensor_tensor(tok_rstd[:, :], tok_var[:, :], minus_half[:, 0:1], ALU.pow).then_inc(s_bnp, 1)

            def rstd(n, b, stats, name):
                done = S[name]
                pool.wait_ge(stats, 2 * TILES * b + 2 * TILES)
                pool.tensor_tensor(ln_var[:, n], ln_mv[:, n, :, 1], eps_sb[:, :], ALU.add).then_inc(done, 1)
                pool.wait_ge(done, NORM * b + 1)
                pool.tensor_tensor(ln_rstd[:, n], ln_var[:, n], minus_half[:, :], ALU.pow).then_inc(done, 1)
                pool.tensor_tensor(ln_nmean[:, n], zeros[:, :], ln_mv[:, n, :, 0], ALU.subtract).then_inc(done, 1)
                pool.wait_ge(done, NORM * b + 3)
                pool.tensor_tensor(ln_shift[:, n], ln_nmean[:, n], ln_rstd[:, n], ALU.mult).then_inc(done, 1)

            def step(i, s0, s1, s2, s3):
                b = i - 1
                if s1:
                    rstd(0, i, S["st1"], "rstd1")
                if s2:
                    rstd(1, b, S["st2"], "rstd2")
                if s1:
                    pool.wait_ge(S["kpos"], i + 1)
                    pool.wait_ge(S["num"], TILES * i)
                    pool.wait_ge(S["ksum"], i)
                    pool.tensor_tensor(k_dec[:, 0:TE], k_pos[:, :], powers[:, 1, 0:TE], ALU.mult
                                       ).then_inc(S["kdec"], 1)
                    pool.wait_ge(S["qpos"], i + 1)
                    pool.wait_ge(S["qks"], i)
                    pool.tensor_tensor(q_dec[:, 0:TE], q_pos[:, :], powers[:, 0, 0:TE], ALU.mult
                                       ).then_inc(S["qdec"], 1)
                if s2:
                    pool.wait_ge(S["projn"], TILES * b + TILES)
                    pool.tensor_tensor(proj_g[:, :, :], proj_n[:, :, :], over_tiles(gamma_row[:, :]), ALU.mult
                                       ).then_inc(S["projg"], 1)
                    pool.wait_ge(S["res"], b + 1)
                    pool.wait_ge(S["projg"], b + 1)
                    pool.tensor_tensor(by_tiles(seqs[:, b]), by_tiles(seqs[:, b]), proj_g[:, :, :], ALU.add
                                       ).then_inc(S["res2"], 1)
                    rstd(2, b, S["st3"], "rstd3")
                if s1:
                    pool.wait_ge(S["qdec"], i + 1)
                    pool.wait_ge(S["ksum"], i + 1)
                    pool.wait_ge(S["den_ps"], i)
                    pool.tensor_tensor(q_ksum[:, 0:TE], q_dec[:, 0:TE], k_sum[:, :], ALU.mult).then_inc(S["qks"], 1)
                if s2:
                    pool.wait_ge(S["x3hi"], b + 1)
                    pool.tensor_tensor(x3_lo[:, :], x3_fm[:, 0:TE], x3_hi[:, :].bitcast(F32), ALU.subtract
                                       ).then_inc(S["x3lo"], 1)
                    route(b)

            def route(b):
                n = 0

                def then(ins, wait=True):
                    nonlocal n
                    n += 1
                    ins.then_inc(S["route"], 1)
                    if wait:
                        pool.wait_ge(S["route"], ROUTE * b + n)

                pool.wait_ge(S["top"], TILES * b + TILES)
                pool.wait_ge(S["expd"], b)
                pool.tensor_tensor(shifted[:, :, :], top8[:, :, :], over_cols(top8[:, :, 0], EXPERTS),
                                   ALU.subtract).then_inc(S["shifted"], 1)
                pool.wait_ge(S["expd"], b + 1)
                then(pool.tensor_tensor(pick_sum[:, :], expd[:, :, 0], expd[:, :, 1], ALU.add), wait=False)
                pool.wait_ge(S["expsum"], b + 1)
                then(pool.tensor_tensor(exp_tiny[:, :], exp_sum[:, :], tiny[:, :], ALU.mult))
                pool.wait_ge(S["pickrec"], b)
                pool.tensor_tensor(pick_den[:, :], exp_tiny[:, :], pick_sum[:, :], ALU.add).then_inc(S["pickden"], 1)
                pool.wait_ge(S["pickrec"], b + 1)
                then(pool.tensor_tensor(top_w[:, :, :], expd[:, :, 0:2], over_cols(pick_rec[:, :], 2), ALU.mult))
                pool.wait_ge(S["istop"], b + 1)
                then(pool.tensor_tensor(placed[:, :, :, :], is_top[:, :, :, :],
                                        top_w[:, :, :].unsqueeze(3).to_broadcast([P, TILES, 2, EXPERTS]), ALU.mult))
                pool.wait_ge(S["combT"], b)
                then(pool.tensor_tensor(comb_parts[:, :, 0], placed[:, :, 0], placed[:, :, 1], ALU.add), wait=False)
                then(pool.tensor_tensor(combine[:, :, :], placed[:, :, 0], placed[:, :, 1], ALU.add))
                then(pool.tensor_tensor(comb_parts[:, :, 1], combine[:, :, :], comb_parts[:, :, 0], ALU.subtract),
                     wait=False)
                then(pool.tensor_tensor(comb_rest[:, :, :], combine[:, :, :], comb_parts[:, :, 0], ALU.subtract))
                assert n == ROUTE
                pool.tensor_tensor(comb_parts[:, :, 2], comb_rest[:, :, :], comb_parts[:, :, 1], ALU.subtract
                                   ).then_inc(S["combine"], 1)

            skewed(pool, step)

        @block.scalar
        def _(act):
            act.wait_ge(s_weights, 16 * WEIGHT_LOADS)
            act.activation(decay[:, 1, 0:1], logits_in[:, :], ACT.Exp, scale=-1.0).then_inc(s_exp0, 1)

            def x_upper(b, j, first):
                act.wait_ge(s_xT, b + 1)
                if not first:
                    act.wait_ge(s_conv, b - 1)
                act.activation(x_hi[:, j, 0:T_IN], (bank_a, bank_b)[j][:, 0:T_IN], ACT.Copy).then_inc(s_xhi, 1)

            def relu_tok(b, j):
                act.wait_ge(s_conv, b + 1)
                act.activation(seqs[:, b, 0:T], (bank_c, bank_d)[j][:, 0:T], ACT.Relu, bias=tok_vec[:, 0:1]
                               ).then_inc(s_relu, 1)

            def turn(pair, first, last):
                x_upper(2 * pair + 1, 1, first)
                relu_tok(2 * pair, 0)
                if not last:
                    x_upper(2 * pair + 2, 0, False)
                relu_tok(2 * pair + 1, 1)

            x_upper(0, 0, True)
            pairs(act, turn)

            def step(i, s0, s1, s2, s3):
                b2_, b3 = i - 1, i - 2

                def relu(e):
                    if not s3:
                        return
                    act.wait_ge(S["l1"], UNITS * b3 + e + 1)
                    if e < EXPERTS:
                        act.wait_ge(S["mix"], EXPERTS * b3 + max(e - 2, 0))
                        dst = hid[:, e % 3]
                    else:
                        act.wait_ge(S["l2"], UNITS * b3 + e - 1)
                        dst = mixed[:, e % 2]
                    act.activation(dst, hid_ps[e % 2][:, 0:TE], ACT.Relu, bias=l1_bias[:, e:e + 1]
                                   ).then_inc(S["hid"], 1)

                def normalize(n, b, dst, src, name, stats):
                    act.wait_ge(S[stats], NORM * b + NORM)
                    for c in range(TILES):
                        act.activation(dst[:, c], src(c), ACT.Identity, bias=ln_shift[:, n, c:c + 1],
                                       scale=ln_rstd[:, n, c:c + 1]).then_inc(S[name], 1)

                relu(0)
                relu(1)
                if s2:
                    act.wait_ge(S["attnT"], b2_ + 1)
                    act.wait_ge(S["proj_ps"], b2_)
                    act.activation(attn[:, :], bank_b[:, 0:TP], ACT.Copy).then_inc(S["attn"], 1)
                relu(2)
                if s1:
                    act.wait_ge(S["xnT"], i)
                    normalize(0, i, xn_tm, lambda c: bank_a[:, c * P:(c + 1) * P], "xn", "rstd1")
                relu(3)
                if s1:
                    act.wait_ge(S["xnT"], i + 1)
                    act.wait_ge(S["v"], i)
                    act.activation(xn_hi[:, :], bank_c[:, 0:TE], ACT.Copy).then_inc(S["xnhi"], 1)
                relu(4)
                if s1:
                    act.wait_ge(S["k"], i + 1)
                    act.activation(k_neg[:, :], bank_b[:, 0:TE], ACT.Relu, bias=qk_nbias[:, 1:2], scale=-1.0
                                   ).then_inc(S["kneg"], 1)
                    act.wait_ge(S["kneg"], i + 1)
                    act.wait_ge(S["kpos"], i)
                    act.activation(k_exp[:, :], k_neg[:, :], ACT.Exp, scale=-1.0).then_inc(S["kexp"], 1)
                    act.wait_ge(S["q"], i + 1)
                    act.activation(q_neg[:, :], bank_a[:, 0:TE], ACT.Relu, bias=qk_nbias[:, 0:1], scale=-1.0
                                   ).then_inc(S["qneg"], 1)
                    act.wait_ge(S["qneg"], i + 1)
                    act.wait_ge(S["qpos"], i)
                    act.activation(q_exp[:, :], q_neg[:, :], ACT.Exp, scale=-1.0).then_inc(S["qexp"], 1)
                    act.wait_ge(S["v"], i + 1)
                    act.wait_ge(S["vT"], i)
                    act.activation(v_fm[:, 0:TE], bank_c[:, 0:TE], ACT.Identity, bias=qkv_bias[:, 2:3]
                                   ).then_inc(S["vfm"], 1)
                relu(5)
                if s2:
                    act.wait_ge(S["projg"], b2_)
                    normalize(1, b2_, proj_n, lambda c: proj[:, c], "projn", "rstd2")
                relu(6)
                if s1:
                    act.wait_ge(S["vT"], i + 1)
                    act.wait_ge(S["num"], TILES * i)
                    act.activation(diagonal(v_par, 0, TILES * PAIRS),
                                   bank_c[:, 0:TP].rearrange("p (g a f) -> p g a f", a=2, f=HD), ACT.Copy
                                   ).then_inc(S["vpar"], 1)
                    act.wait_ge(S["kT"], i + 1)
                    act.wait_ge(S["mem_ps"], i)
                    act.activation(k_tm[:, :, :], bank_d[:, 0:(TILES - 1) * P].rearrange("p (c n) -> p c n", n=P),
                                   ACT.Copy).then_inc(S["ktm"], 1)
                    act.wait_ge(S["qdec"], i + 1)
                    act.wait_ge(S["sc_ps"], 2 * TILES * i)
                    for m in (0, 1):
                        act.activation(q_one[:, m, 0:TE], q_dec[:, 0:TE], ACT.Copy, scale=head_mod[:, m:m + 1]
                                       ).then_inc(S["qone"], 1)
                relu(7)
                relu(8)
                if s2:
                    act.wait_ge(S["x3T"], b2_)
                    normalize(2, b2_, x3_tm, lambda c: seqs[:, b2_, c * P:(c + 1) * P], "x3", "rstd3")
                    act.wait_ge(S["x3T"], b2_ + 1)
                    act.wait_ge(S["x3lo"], b2_)
                    act.activation(x3_fm[:, :], bank_b[:, 0:TP], ACT.Copy).then_inc(S["x3fm"], 1)
                    act.activation(x3_hi[:, :], bank_b[:, 0:TE], ACT.Copy).then_inc(S["x3hi"], 1)
                    act.wait_ge(S["shifted"], b2_ + 1)
                    act.wait_ge(S["route"], ROUTE * b2_)
                    act.activation(expd[:, :, :], shifted[:, :, :], ACT.Exp).then_inc(S["expd"], 1)
                if s1:
                    act.wait_ge(S["num"], TILES * i + TILES)
                    act.wait_ge(S["numT"], i)
                    act.activation(num_sb[:, :], bank_d[:, 0:TP], ACT.Copy).then_inc(S["numsb"], 1)
                if s3:
                    act.wait_ge(S["ydone"], b3 + 1)
                    act.wait_ge(S["yT"], b3)
                    act.activation(y_fm[:, 0:TE], y_ps[:, 0:TE], ACT.Identity, bias=l2_bias[:, 0:1]
                                   ).then_inc(S["yfm"], 1)

            skewed(act, step)

        @block.tensor
        def _(pe):
            pe.wait_ge(s_const, CONSTS)
            pe.wait_ge(s_tokw, 16)
            for i in range(TAPS):
                dst = bank_c[:, i * P:(i + 1) * P] if i < 4 else bank_d[:, 0:P]
                pe.transpose(dst, tok_w_raw[:, i], ident[:, :]).then_inc(s_wt_ps, 1)

            def transpose_x(pair, j, first):
                pe.wait_ge(s_x[j], 16 * pair + 16)
                if not first:
                    pe.wait_ge(s_xlo, 2 * pair + j - 1)
                for c in range(TILES):
                    ins = pe.transpose((bank_a, bank_b)[j][:, c * XROWS:(c + 1) * XROWS], x_in[0:XROWS, j, c],
                                       ident[0:XROWS, 0:XROWS])
                ins.then_inc(s_xT, 1)

            def conv(pair, j, first):
                b = 2 * pair + j
                pe.wait_ge(s_xlo, b + 1)
                if not first:
                    pe.wait_ge(s_relu, b - 1)
                for i in range(TAPS):
                    ins = split3(pe, (bank_c, bank_d)[j][:, 0:TE], tok_hi[:, i], tok_lo[:, i],
                                 x_hi[:, j, i:i + TE], x_lo[:, j, i:i + TE], i == 0, i == TAPS - 1)
                ins.then_inc(s_conv, 1)

            def turn(pair, first, last):
                transpose_x(pair, 1, first)
                conv(pair, 0, first)
                if not last:
                    transpose_x(pair + 1, 0, False)
                conv(pair, 1, first)

            pe.wait_ge(s_cvec, CVEC_TOK)
            transpose_x(0, 0, True)
            pairs(pe, turn)

            pe.wait_ge(s_weights, 16 * WEIGHT_LOADS)
            pe.wait_ge(s_stat, B)
            pe.transpose(bank_a[:, 0:EXPERTS], gate_raw[:, :], ident[0:EXPERTS, 0:EXPERTS]).then_inc(s_wt_ps, 1)
            pe.wait_ge(s_cvec, CVEC_ALL)

            def tile(t, c):
                return t[:, c * P:(c + 1) * P]

            def step(i, s0, s1, s2, s3):
                b2_, b3 = i - 1, i - 2
                fixed = isinstance(i, int)

                def unit(e):
                    if not s3:
                        return
                    if e < UNITS:
                        pe.wait_ge(S["hid"], UNITS * b3 + max(e - 1, 0))
                        if e == 0:
                            pe.wait_ge(S["x3lo"], b3 + 1)
                        split3(pe, hid_ps[e % 2][:, 0:TE], l1_hi[:, e], l1_lo[:, e], x3_hi[:, :], x3_lo[:, :],
                               True, True).then_inc(S["l1"], 1)
                    w = e - 2
                    if 0 <= w < EXPERTS:
                        if w == 0:
                            pe.wait_ge(S["combfm"], b3 + 1)
                        pe.wait_ge(S["mix"], EXPERTS * b3 + w)
                        pe.matmul(comb_ps[:, 0:TE], part_select[:, w], comb_fm[:, 0:TE], start=True, stop=True
                                  ).then_inc(S["cb"], 1)
                    f = e - 3
                    if 0 <= f < UNITS:
                        if f == 0:
                            pe.wait_ge(S["yfm"], b3)
                        if f < EXPERTS:
                            pe.wait_ge(S["mix"], EXPERTS * b3 + f + 1)
                        else:
                            pe.wait_ge(S["hid"], UNITS * b3 + UNITS)
                        pe.matmul(y_ps[:, 0:TE], l2_w[:, f], mixed[:, f % 2], start=(f == 0), stop=False
                                  ).then_inc(S["l2"], 1)
                    if f == UNITS - 1:
                        for n in range(PARTS):
                            ins = pe.matmul(y_ps[:, 0:TE], b2_parts[:, n], comb_fm[:, 0:TE], start=False,
                                            stop=(n == PARTS - 1))
                        ins.then_inc(S["ydone"], 1)

                def attend(c):
                    pe.wait_ge(S["sc"], 2 * TILES * i + 2 * c + 2)
                    dst = tile(bank_d, c)
                    if c:
                        pe.matmul(dst, memory[:, c - 1], tile(q_dec, c), start=True, stop=True)
                    for a in range(2):
                        for g in range(PAIRS):
                            rows = slice(2 * HD * g, 2 * HD * (g + 1))
                            ins = pe.matmul(bank_d[rows, c * P:(c + 1) * P], v_par[:, c * PAIRS + g, a],
                                            scores[:, c, 2 * g + a], start=(c == 0 and a == 0),
                                            stop=(c > 0 or a == 1), skip_group_check=(c > 0))
                    ins.then_inc(S["num"], 1)

                def score(c, half, dst):
                    rows = slice(64 * half, 64 * half + 64)
                    pe.matmul(dst[:, :].rearrange("p (m t) -> p m t", m=HALF), k_dec[rows, c * P:(c + 1) * P],
                              q_one[rows, :, c * P:(c + 1) * P], start=True, stop=True).then_inc(S["sc_ps"], 1)

                if s1:
                    pe.wait_ge(S["hfm"], i + 1)
                    pe.wait_ge(S["den"], i)
                    for c in range(TILES):
                        ins = pe.transpose(tile(bank_a, c), tile(h_fm, c), ident[:, :])
                    ins.then_inc(S["hT"], 1)
                if s2:
                    pe.wait_ge(S["numsb"], b2_ + 1)
                    for c in range(TILES):
                        ins = pe.transpose(tile(bank_d, c), tile(num_sb, c), ident[:, :])
                    ins.then_inc(S["numT"], 1)
                unit(0)
                unit(1)
                if s2:
                    pe.wait_ge(S["attntm"], b2_ + 1)
                    pe.wait_ge(S["x3hi"], b2_)
                    if not fixed or i > 2:
                        pe.wait_ge(S["outsb"], i - 2)
                    for c in range(TILES):
                        ins = pe.transpose(tile(bank_b, c), attn_tm[:, c], ident[:, :])
                    ins.then_inc(S["attnT"], 1)
                if s3:
                    pe.wait_ge(S["combine"], b3 + 1)
                    comb_t = bank_c[:, :].bitcast(BF16)
                    for c in range(TILES):
                        ins = pe.transpose(comb_t[0:PARTS * EXPERTS, c * P:(c + 1) * P],
                                           comb_parts[:, c].rearrange("p n e -> p (n e)"), ident_bf[:, :])
                    ins.then_inc(S["combT"], 1)
                unit(2)
                unit(3)
                if s1:
                    pe.wait_ge(S["xn"], TILES * i + TILES)
                    if s3:
                        pe.wait_ge(S["combfm"], b3 + 1)
                    elif i:
                        pe.wait_ge(S["sc"], 2 * TILES * i)
                    for c in range(TILES):
                        ins = pe.transpose(tile(bank_c, c), xn_tm[:, c], ident[:, :])
                    ins.then_inc(S["xnT"], 1)
                if s2:
                    pe.wait_ge(S["attn"], b2_ + 1)
                    for c in range(TILES):
                        ins = pe.matmul(tile(bank_d, c), tile(attn, c), wout_sb[:, :], start=True, stop=True)
                    ins.then_inc(S["proj_ps"], 1)
                unit(4)
                if s1:
                    pe.wait_ge(S["xnlo"], i + 1)
                    for n, (dst, name) in ((1, (bank_b, "k")), (0, (bank_a, "q")), (2, (bank_c, "v"))):
                        if n == 0:
                            pe.wait_ge(S["res"], i + 1)
                        split3(pe, dst[:, 0:TE], qkv_hi[:, n], qkv_lo[:, n], xn_hi[:, :], xn_lo[:, :], True, True
                               ).then_inc(S[name], 1)
                unit(5)
                if s1:
                    pe.wait_ge(S["vfm"], i + 1)
                    for c in range(TILES):
                        ins = pe.transpose(tile(bank_c, c), tile(v_fm, c), ident[:, :])
                    ins.then_inc(S["vT"], 1)
                unit(6)
                if s1:
                    pe.wait_ge(S["kdec"], i + 1)
                    if s2:
                        pe.wait_ge(S["proj"], b2_ + 1)
                    for c in range(TILES - 1):
                        ins = pe.transpose(tile(bank_d, c), tile(k_dec, c), ident[:, :])
                    ins.then_inc(S["kT"], 1)
                unit(7)
                if s1:
                    pe.wait_ge(S["ktm"], i + 1)
                    pe.wait_ge(S["vpar"], i + 1)
                    pe.wait_ge(S["qpos"], i + 1)
                    for n in range(TILES - 1):
                        for c in range(n + 1):
                            ins = pe.matmul(tile(bank_a, n), k_tm[:, c], diagonal(v_par, c * PAIRS, PAIRS),
                                            start=(c == 0), stop=(c == n))
                    ins.then_inc(S["mem_ps"], 1)
                    pe.wait_ge(S["qone"], 2 * i + 2)
                    pe.wait_ge(S["qone2"], 2 * i + 2)
                    score(0, 0, bank_b)
                    score(0, 1, bank_c)
                unit(8)
                if s1:
                    pe.wait_ge(S["mem"], i + 1)
                    score(1, 0, bank_a)
                    pe.wait_ge(S["sc"], 2 * TILES * i + 1)
                    score(1, 1, bank_b)
                    attend(0)
                unit(9)
                if s1:
                    score(2, 0, bank_c)
                    pe.wait_ge(S["sc"], 2 * TILES * i + 3)
                    score(2, 1, bank_a)
                if s2:
                    pe.wait_ge(S["x3"], TILES * b2_ + TILES)
                    if s1:
                        pe.wait_ge(S["sc"], 2 * TILES * i + 4)
                    for c in range(TILES):
                        ins = pe.transpose(tile(bank_b, c), x3_tm[:, c], ident[:, :])
                    ins.then_inc(S["x3T"], 1)
                if s1:
                    attend(1)
                if s2:
                    pe.wait_ge(S["x3fm"], b2_ + 1)
                    if s1:
                        pe.wait_ge(S["sc"], 2 * TILES * i + 5)
                    for c in range(TILES):
                        ins = pe.matmul(tile(bank_c, c)[:, 0:GATE_COLS], tile(x3_fm, c), gate[:, :],
                                        start=True, stop=True)
                    ins.then_inc(S["gate_ps"], 1)
                unit(10)
                if s1:
                    attend(2)
                unit(11)
                if s1:
                    pe.wait_ge(S["qks"], i + 1)
                    for c in range(TILES):
                        ins = pe.matmul(tile(bank_a, c)[:, 0:GATE_COLS], tile(q_ksum, c), head_sum[:, :],
                                        start=True, stop=True)
                    ins.then_inc(S["den_ps"], 1)
                if s3:
                    pe.wait_ge(S["yfm"], b3 + 1)
                    if s2:
                        pe.wait_ge(S["x3hi"], b2_ + 1)
                    else:
                        pe.wait_ge(S["outsb"], b3)
                    for c in range(TILES):
                        ins = pe.transpose(tile(bank_b, c), tile(y_fm, c), ident[:, :])
                    ins.then_inc(S["yT"], 1)

            skewed(pe, step)

        @block.vector
        def _(dve):
            done = 0

            def link(ins):
                nonlocal done
                done += 1
                ins.then_inc(s_cvec, 1)
                dve.wait_ge(s_cvec, done)

            def halves(hi, lo, src):
                link(dve.tensor_copy(hi, src))
                link(dve.tensor_tensor(lo, src, hi.bitcast(F32), ALU.subtract))

            dve.wait_ge(s_const, CONSTS)
            dve.wait_ge(s_wt_ps, TAPS)
            link(dve.tensor_copy(tok_wf[:, 0:4], bank_c[:, :].rearrange("p (i n) -> p i n", n=P)))
            link(dve.tensor_copy(tok_wf[:, 4], bank_d[:, 0:P]))
            halves(tok_hi[:, :, :], tok_lo[:, :, :], tok_wf[:, :, :])
            link(dve.tensor_scalar(x_hi[:, :, T_IN:XW], ones[:, 0:2 * (XW - T_IN)].rearrange(
                "p (a n) -> p a n", a=2), 0.0, None, ALU.mult))
            link(dve.tensor_scalar(x_lo[:, :, T_IN:XW], ones[:, 0:2 * (XW - T_IN)].rearrange(
                "p (a n) -> p a n", a=2), 0.0, None, ALU.mult))
            assert done == CVEC_TOK

            def x_lower(b, j, first):
                dve.wait_ge(s_xhi, b + 1)
                dve.tensor_tensor(x_lo[:, j, 0:T_IN], (bank_a, bank_b)[j][:, 0:T_IN],
                                  x_hi[:, j, 0:T_IN].bitcast(F32), ALU.subtract).then_inc(s_xlo, 1)

            def stats_tok(b):
                dve.wait_ge(s_relu, b + 1)
                dve.bn_stats(tok_stats[:, b], seqs[:, b, 0:T]).then_inc(s_stat, 1)

            def turn(pair, first, last):
                x_lower(2 * pair + 1, 1, first)
                stats_tok(2 * pair)
                if not last:
                    x_lower(2 * pair + 2, 0, False)
                stats_tok(2 * pair + 1)
                if first:
                    prepare()

            def prepare():
                dve.wait_ge(s_weights, 16 * WEIGHT_LOADS)
                halves(qkv_hi[:, :, :], qkv_lo[:, :, :], qkv_raw[:, :, :])
                halves(l1_hi[:, :, :], l1_lo[:, :, :], l1_raw[:, :, :])
                link(dve.tensor_scalar(qk_bias1[:, :], qkv_bias[:, 0:2], 1.0, None, ALU.add))
                link(dve.tensor_scalar(qk_nbias[:, :], qkv_bias[:, 0:2], -1.0, None, ALU.mult))
                link(dve.tensor_copy(ident_bf[:, :], ident[:, :]))
                hm = head_block[:, :].rearrange("p (h e) -> p h e", h=HEADS)
                link(dve.tensor_tensor(head_mod[:, :], hm[:, 0:HALF, 0], hm[:, HALF:HEADS, 0], ALU.add))
                link(dve.tensor_copy(head_sum[:, 0:HEADS], hm[:, :, 0]))
                link(dve.tensor_copy(b2_parts[:, 0], b2_raw[:, :]))
                link(dve.tensor_tensor(b2_rest[:, 0], b2_raw[:, :], b2_parts[:, 0], ALU.subtract))
                link(dve.tensor_copy(b2_parts[:, 1], b2_rest[:, 0]))
                link(dve.tensor_tensor(b2_rest[:, 1], b2_rest[:, 0], b2_parts[:, 1], ALU.subtract))
                link(dve.tensor_copy(b2_parts[:, 2], b2_rest[:, 1]))
                dve.wait_ge(s_exp0, 1)
                link(dve.tensor_scalar(decay[:, 1, 0:1], decay[:, 1, 0:1], 1.0, None, ALU.add))
                link(dve.reciprocal(decay[:, 0, 0:1], decay[:, 1, 0:1]))
                link(dve.tensor_copy(powers[:, :, 0:1], ones[:, 0:2].unsqueeze(2)))
                for n in range(9):
                    w = 1 << n
                    for a in range(2):
                        link(dve.tensor_scalar(powers[:, a, w:2 * w], powers[:, a, 0:w], decay[:, a, n:n + 1], None,
                                               ALU.mult))
                    link(dve.tensor_tensor(decay[:, :, n + 1], decay[:, :, n], decay[:, :, n], ALU.mult))

            x_lower(0, 0, True)
            pairs(dve, turn)

            dve.wait_ge(s_wt_ps, TAPS + 1)
            link(dve.tensor_copy(gate[:, 0:EXPERTS], bank_a[:, 0:EXPERTS]))
            dve.wait_ge(s_stat, B)
            dve.bn_aggr(tok_mv[:, :], tok_stats[:, :, :].rearrange("p b s -> p (b s)")).then_inc(s_bn, 1)
            dve.wait_ge(s_bnp, 2)
            link(dve.tensor_tensor(bn_scale[:, :], tok_vec[:, 1:2], tok_rstd[:, :], ALU.mult))
            link(dve.tensor_scalar(bn_shift[:, :], tok_mv[:, 0:1], bn_scale[:, 0:1], tok_vec[:, 2:3],
                                   ALU.mult, ALU.subtract))
            assert done == CVEC_ALL

            def norm_stats(n, b, src, name):
                s = S[name]
                for c in range(TILES):
                    dve.bn_stats(ln_stats[:, n, c], src(c)).then_inc(s, 1)
                for c in range(TILES):
                    if c == 0:
                        dve.wait_ge(s, 2 * TILES * b + TILES)
                        dve.memset(fence[:, :], 0.0)
                    dve.bn_aggr(ln_mv[:, n, c], ln_stats[:, n, c]).then_inc(s, 1)

            def step(i, s0, s1, s2, s3):
                b2_, b3 = i - 1, i - 2
                fixed = isinstance(i, int)

                def tile_a(c):
                    return bank_a[:, c * P:(c + 1) * P]

                def mix(e):
                    if not s3:
                        return
                    dve.wait_ge(S["hid"], UNITS * b3 + e + 1)
                    dve.wait_ge(S["l2"], UNITS * b3 + max(e - 1, 0))
                    dve.wait_ge(S["cb"], EXPERTS * b3 + e + 1)
                    dve.tensor_tensor(mixed[:, e % 2], hid[:, e % 3], comb_ps[:, 0:TE], ALU.mult
                                      ).then_inc(S["mix"], 1)

                def take_scores(c, n, src):
                    dve.wait_ge(S["sc_ps"], 2 * TILES * i + 2 * c + n + 1)
                    dve.tensor_tensor(scores[:, c, HALF * n:HALF * (n + 1)],
                                      src[:, :].rearrange("p (m t) -> p m t", m=HALF),
                                      causal[:, :].unsqueeze(1).to_broadcast([P, HALF, P]), ALU.mult
                                      ).then_inc(S["sc"], 1)

                if s1:
                    dve.wait_ge(S["hT"], i + 1)
                    norm_stats(0, i, tile_a, "st1")
                if s2:
                    dve.wait_ge(S["attnT"], b2_)
                    dve.wait_ge(S["rden"], b2_ + 1)
                    dve.wait_ge(S["numT"], b2_ + 1)
                    dve.tensor_tensor(attn_tm[:, :, :].rearrange("p c (h e) -> p c h e", h=HEADS),
                                      bank_d[:, 0:TP].rearrange("p (c h e) -> p c h e", c=TILES, h=HEADS),
                                      rden[:, :, :].unsqueeze(3).to_broadcast([P, TILES, HEADS, HD]), ALU.mult
                                      ).then_inc(S["attntm"], 1)
                if s3:
                    dve.wait_ge(S["ydone"], b3)
                    dve.wait_ge(S["combT"], b3 + 1)
                    dve.tensor_copy(comb_fm[:, :], bank_c[:, :].bitcast(BF16)[0:PARTS * EXPERTS, 0:TP]
                                    ).then_inc(S["combfm"], 1)
                mix(0)
                if s1:
                    dve.wait_ge(S["xn"], TILES * i + TILES)
                    dve.tensor_tensor(by_tiles(seqs[:, i]), bank_a[:, 0:TP].rearrange("p (c n) -> p c n", n=P),
                                      over_tiles(beta_row[:, :]), ALU.add).then_inc(S["res"], 1)
                if s1:
                    dve.wait_ge(S["xnhi"], i + 1)
                    dve.tensor_tensor(xn_lo[:, :], bank_c[:, 0:TE], xn_hi[:, :].bitcast(F32), ALU.subtract
                                      ).then_inc(S["xnlo"], 1)
                mix(1)
                if s2:
                    dve.wait_ge(S["projn"], TILES * b2_)
                    dve.wait_ge(S["proj_ps"], b2_ + 1)
                    dve.tensor_tensor(proj[:, :, :], bank_d[:, 0:TP].rearrange("p (c n) -> p c n", n=P),
                                      over_tiles(bout_row[:, :]), ALU.add).then_inc(S["proj"], 1)
                    dve.wait_ge(S["proj"], b2_ + 1)
                    norm_stats(1, b2_, lambda c: proj[:, c], "st2")
                mix(2)
                if s1:
                    dve.wait_ge(S["kdec"], i)
                    dve.wait_ge(S["kexp"], i + 1)
                    dve.scalar_tensor_tensor(out=k_pos[:, :], in0=bank_b[:, 0:TE], scalar=qk_bias1[:, 1:2],
                                             in1=k_exp[:, :], op0=ALU.add, op1=ALU.max).then_inc(S["kpos"], 1)
                    dve.wait_ge(S["qdec"], i)
                    dve.wait_ge(S["qexp"], i + 1)
                    dve.scalar_tensor_tensor(out=q_pos[:, :], in0=bank_a[:, 0:TE], scalar=qk_bias1[:, 0:1],
                                             in1=q_exp[:, :], op0=ALU.add, op1=ALU.max).then_inc(S["qpos"], 1)
                mix(3)
                if s0:
                    dve.tensor_scalar(h_fm[:, 0:T], seqs[:, i + 1, 0:T], bn_scale[:, 0:1], bn_shift[:, 0:1],
                                      ALU.mult, ALU.subtract).then_inc(S["hfm"], 1)
                if s1:
                    dve.wait_ge(S["qks"], i)
                    dve.wait_ge(S["kdec"], i + 1)
                    dve.tensor_tensor_scan(k_sum[:, :], ones[:, 0:TE], k_dec[:, 0:TE], 0.0, ALU.mult, ALU.add
                                           ).then_inc(S["ksum"], 1)
                mix(4)
                if s1:
                    dve.wait_ge(S["sc_ps"], 2 * TILES * i)
                    dve.wait_ge(S["qdec"], i + 1)
                    for m in (2, 3):
                        dve.tensor_scalar(q_one[:, m, 0:TE], q_dec[:, 0:TE], head_mod[:, m:m + 1], None, ALU.mult
                                          ).then_inc(S["qone2"], 1)
                mix(5)
                if s1:
                    dve.wait_ge(S["mem_ps"], i + 1)
                    dve.wait_ge(S["num"], TILES * i)
                    dve.tensor_tensor(memory[:, :, :], bank_a[:, 0:2 * P].rearrange("p (n m) -> p n m", n=2),
                                      head_block[:, :].unsqueeze(1).to_broadcast([P, 2, P]), ALU.mult
                                      ).then_inc(S["mem"], 1)
                if s2:
                    dve.wait_ge(S["res2"], b2_ + 1)
                    norm_stats(2, b2_, lambda c: seqs[:, b2_, c * P:(c + 1) * P], "st3")
                if s1:
                    take_scores(0, 0, bank_b)
                    take_scores(0, 1, bank_c)
                mix(6)
                if s1:
                    take_scores(1, 0, bank_a)
                    take_scores(1, 1, bank_b)
                    take_scores(2, 0, bank_c)
                mix(7)
                if s1:
                    take_scores(2, 1, bank_a)
                if s2:
                    find_top(b2_)
                    dve.wait_ge(S["expd"], b2_ + 1)
                    dve.wait_ge(S["route"], ROUTE * b2_)
                    dve.tensor_reduce(exp_sum[:, :], expd[:, :, :], AX_X, ALU.add).then_inc(S["expsum"], 1)
                    dve.wait_ge(S["pickden"], b2_ + 1)
                    dve.reciprocal(pick_rec[:, :], pick_den[:, :]).then_inc(S["pickrec"], 1)
                if s1:
                    dve.wait_ge(S["den_ps"], i + 1)
                    dve.wait_ge(S["rden"], i)
                    dve.tensor_scalar(den_tm[:, :, :], bank_a[:, 0:TP].rearrange("p (c n) -> p c n", n=P)[:, :, 0:HEADS],
                                      DEN_EPS * HD ** 0.5, None, ALU.add).then_inc(S["den"], 1)
                    dve.wait_ge(S["den"], i + 1)
                    dve.wait_ge(S["attntm"], i)
                    dve.reciprocal(rden[:, :, :], den_tm[:, :, :]).then_inc(S["rden"], 1)
                if s3:
                    dve.wait_ge(S["store"], 32 * b3)
                    dve.wait_ge(S["yT"], b3 + 1)
                    dve.tensor_tensor(out_sb[:, :, :], bank_b[:, 0:TP].rearrange("p (c n) -> p c n", n=P),
                                      by_tiles(seqs[:, b3]), ALU.add).then_inc(S["outsb"], 1)

            def find_top(b):
                gate_out = bank_c[:, 0:TP].rearrange("p (c n) -> p c n", n=P)[:, :, 0:EXPERTS]
                dve.wait_ge(S["gate_ps"], b + 1)
                dve.wait_ge(S["shifted"], b)
                dve.memset(fence[:, :], 0.0)
                for c in range(TILES):
                    dve.max(top8[:, c], gate_out[:, c]).then_inc(S["top"], 1)
                dve.wait_ge(S["top"], TILES * b + TILES)
                dve.memset(fence[:, :], 0.0)
                for c in range(TILES):
                    dve.max_index(top_at[:, c], top8[:, c], gate_out[:, c]).then_inc(S["topat"], 1)
                dve.wait_ge(S["topat"], TILES * b + TILES)
                dve.wait_ge(S["combine"], b)
                dve.tensor_tensor(is_top[:, :, :, :],
                                  expert_ids[:, :].unsqueeze(1).unsqueeze(1).to_broadcast([P, TILES, 2, EXPERTS]),
                                  top_at[:, :, 0:2].unsqueeze(3).to_broadcast([P, TILES, 2, EXPERTS]), ALU.is_equal
                                  ).then_inc(S["istop"], 1)

            skewed(dve, step)


CONSTS = 19 + 8 + 4 + PARTS
WEIGHT_LOADS = 18 + PARTS
CVEC_TOK = 6
CVEC_ALL = 6 + 4 + 5 + 5 + 3 + 27 + 1 + 2
NORM = 4
ROUTE = 8

_INS = ["x", "L0_tok_W", "L0_tok_b", "L0_tok_gamma", "L0_tok_beta", "L0_attn_Wqkv", "L0_attn_bqkv",
        "L0_attn_Wout", "L0_attn_bout", "L0_attn_ln_gamma", "L0_attn_ln_beta", "L0_attn_decay_logits",
        "L0_ffn_gate_w", "L0_ffn_w1", "L0_ffn_b1", "L0_ffn_w2", "L0_ffn_b2", "L0_ffn_sw1", "L0_ffn_sb1",
        "L0_ffn_sw2", "L0_ffn_sb2"]


def kernel(**inputs):
    import numpy as np
    import concourse.bacc as bacc
    from concourse.bass_utils import run_bass_kernel_spmd

    nc = bacc.Bacc("TRN2", target_bir_lowering=False, num_devices=1)
    arrays, args = {}, []
    for name in _INS:
        a = np.ascontiguousarray(inputs[name])
        arrays[f"in_{name}"] = a
        args.append(nc.dram_tensor(f"in_{name}", a.shape, mybir.dt.from_np(a.dtype), kind="ExternalInput").ap())
    b, t, d = inputs["x"].shape
    args.append(nc.dram_tensor("out", (b, t - (TAPS - 1), d), F32, kind="ExternalOutput").ap())
    build(nc, *args)
    r = run_bass_kernel_spmd(nc, [arrays], core_ids=[0])
    return r.results[0]["out"]
```

```python
from contextlib import ExitStack

import concourse.bass as bass
from concourse import mybir

F32 = mybir.dt.float32
F32R = mybir.dt.float32r
BF16 = mybir.dt.bfloat16
U32 = mybir.dt.uint32
ALU = mybir.AluOpType
ACT = mybir.ActivationFunctionType
AX_X = mybir.AxisListType.X

P = 128
TAPS = 5
HEADS = 8
HD = P // HEADS
PAIRS = HEADS // 2
HALF = HEADS // 2
EXPERTS = 8
UNITS = EXPERTS + 1
QUAD = 4
PARTS = 3
GATE_COLS = 96
EPS = 1e-5
DEN_EPS = 1e-5


def build(nc, x, tok_w, tok_b, tok_gamma, tok_beta, wqkv, bqkv, wout, bout, ln_gamma, ln_beta,
          decay_logits, gate_w, w1, b1, w2, b2, sw1, sb1, sw2, sb2, out):
    B, T_IN, _ = x.shape
    T = T_IN - (TAPS - 1)
    TILES = -(-T // P)
    TP = TILES * P
    TE = T + T % 2
    XROWS = T_IN // TILES
    XW = TE + TAPS - 1
    LAST = T - (TILES - 1) * P
    assert T_IN == XROWS * TILES and B % QUAD == 0 and TP <= 512

    with ExitStack() as ctx:
        def sb(name, shape, dt=F32):
            return ctx.enter_context(nc.sbuf_tensor(name, shape, dt))

        def bank(name):
            return ctx.enter_context(nc.psum_tensor(name, [P, 512], F32))

        def sem(name):
            return ctx.enter_context(nc.semaphore(name))

        ident = sb("ident", [P, P])
        ident_bf = sb("ident_bf", [P, P], BF16)
        causal = sb("causal", [P, P])
        head_block = sb("head_block", [P, P])
        head_mod = sb("head_mod", [P, HALF])
        ones = sb("ones", [P, TP])
        minus_half = sb("minus_half", [P, TILES])
        expert_ids = sb("expert_ids", [P, EXPERTS])
        part_select = sb("part_select", [PARTS * EXPERTS, EXPERTS, P], BF16)
        tok_w_raw = sb("tok_w_raw", [P, TAPS, P])
        gate_raw = sb("gate_raw", [EXPERTS, P])
        gate = sb("gate", [P, GATE_COLS])
        wout_sb = sb("wout_sb", [P, P])
        tok_hi = sb("tok_hi", [P, TAPS, P], F32R)
        tok_lo = sb("tok_lo", [P, TAPS, P], F32R)
        qkv_hi = sb("qkv_hi", [P, 3, P], F32R)
        qkv_lo = sb("qkv_lo", [P, 3, P], F32R)
        l1_hi = sb("l1_hi", [P, UNITS, P], F32R)
        l1_lo = sb("l1_lo", [P, UNITS, P], F32R)
        l2_hi = sb("l2_hi", [P, UNITS, P], F32R)
        l2_lo = sb("l2_lo", [P, UNITS, P], F32R)
        b2_raw = sb("b2_raw", [PARTS * EXPERTS, P])
        b2_rest = sb("b2_rest", [PARTS * EXPERTS, 2, P])
        b2_parts = sb("b2_parts", [PARTS * EXPERTS, PARTS, P], BF16)
        l1_bias = sb("l1_bias", [P, UNITS])
        l2_bias = sb("l2_bias", [P, 1])
        tok_vec = sb("tok_vec", [P, 3])
        qkv_bias = sb("qkv_bias", [P, 3])
        qk_bias1 = sb("qk_bias1", [P, 2])
        qk_nbias = sb("qk_nbias", [P, 2])
        head_sum = sb("head_sum", [P, GATE_COLS])
        tiny = sb("tiny", [P, TILES])
        zeros = sb("zeros", [P, TILES])
        eps_sb = sb("eps_sb", [P, TILES])
        fence = sb("fence", [P, 6])
        bout_row = sb("bout_row", [P, P])
        gamma_row = sb("gamma_row", [P, P])
        beta_row = sb("beta_row", [P, P])
        logits_in = sb("logits_in", [P, 1])
        decay = sb("decay", [P, 2, 10])
        powers = sb("powers", [P, 2, 512])

        x_in = sb("x_in", [P, QUAD, TILES, P])
        x_hi = sb("x_hi", [P, 2, XW], F32R)
        x_lo = sb("x_lo", [P, 2, XW], F32R)
        seqs = sb("seqs", [P, B, TP])
        tok_stats = sb("tok_stats", [P, B, 6])
        tok_mv = sb("tok_mv", [P, 2])
        tok_var = sb("tok_var", [P, 1])
        tok_rstd = sb("tok_rstd", [P, 1])
        bn_scale = sb("bn_scale", [P, 1])
        bn_shift = sb("bn_shift", [P, 1])

        h_fm = sb("h_fm", [P, TP])
        ln_stats = sb("ln_stats", [P, 3, TILES, 6])
        ln_mv = sb("ln_mv", [P, 3, TILES, 2])
        ln_var = sb("ln_var", [P, 3, TILES])
        ln_rstd = sb("ln_rstd", [P, 3, TILES])
        ln_nmean = sb("ln_nmean", [P, 3, TILES])
        ln_shift = sb("ln_shift", [P, 3, TILES])
        xn_tm = sb("xn_tm", [P, TILES, P])
        xn_hi = sb("xn_hi", [P, TE], F32R)
        xn_lo = sb("xn_lo", [P, TE], F32R)
        q_exp = sb("q_exp", [P, TE])
        k_exp = sb("k_exp", [P, TE])
        q_neg = sb("q_neg", [P, TE])
        k_neg = sb("k_neg", [P, TE])
        q_pos = sb("q_pos", [P, TE])
        k_pos = sb("k_pos", [P, TE])
        q_dec = sb("q_dec", [P, TP])
        k_dec = sb("k_dec", [P, TP])
        q_one = sb("q_one", [P, HALF, TP])
        v_fm = sb("v_fm", [P, TP])
        k_sum = sb("k_sum", [P, TE])
        q_ksum = sb("q_ksum", [P, TP])
        k_tm = sb("k_tm", [P, TILES - 1, P])
        v_par = sb("v_par", [P, TILES * PAIRS, 2, 2 * HD])
        memory = sb("memory", [P, 2, P])
        scores = sb("scores", [P, TILES, HEADS, P])
        raw = scores[:, :, :, :].rearrange("p c h n -> p (c h) n")
        l1_raw, l2_raw, qkv_raw = raw[:, 0:UNITS], raw[:, UNITS:2 * UNITS], raw[:, 2 * UNITS:2 * UNITS + 3]
        assert 2 * UNITS + 3 <= TILES * HEADS
        num_sb = sb("num_sb", [P, TP])
        den_tm = sb("den_tm", [P, TILES, HEADS])
        rden = sb("rden", [P, TILES, HEADS])
        attn_tm = sb("attn_tm", [P, TILES, P])
        attn = sb("attn", [P, TP])

        proj = sb("proj", [P, TILES, P])
        proj_g = sb("proj_g", [P, TILES, P])
        x3_tm = sb("x3_tm", [P, TILES, P])
        x3_fm = sb("x3_fm", [P, TP])
        x3_hi = sb("x3_hi", [P, TE], F32R)
        x3_lo = sb("x3_lo", [P, TE], F32R)
        top8 = sb("top8", [P, TILES, 8])
        top_at = sb("top_at", [P, TILES, 8], U32)
        is_top = sb("is_top", [P, TILES, 2, EXPERTS])
        shifted = sb("shifted", [P, TILES, EXPERTS])
        expd = sb("expd", [P, TILES, EXPERTS])
        exp_sum = sb("exp_sum", [P, TILES])
        exp_tiny = sb("exp_tiny", [P, TILES])
        pick_sum = sb("pick_sum", [P, TILES])
        pick_den = sb("pick_den", [P, TILES])
        pick_rec = sb("pick_rec", [P, TILES])
        top_w = sb("top_w", [P, TILES, 2])
        placed = sb("placed", [P, TILES, 2, EXPERTS])
        combine = sb("combine", [P, TILES, EXPERTS])
        comb_rest = sb("comb_rest", [P, TILES, EXPERTS])
        comb_parts = sb("comb_parts", [P, TILES, PARTS, EXPERTS], BF16)

        comb_fm = sb("comb_fm", [PARTS * EXPERTS, TP], BF16)
        hid = sb("hid", [P, 3, TE])
        mixed = sb("mixed", [P, 3, TE])
        mixed_hi = sb("mixed_hi", [P, 4, TE], F32R)
        mixed_lo = sb("mixed_lo", [P, 4, TE], F32R)
        y_fm = sb("y_fm", [P, TP])
        out_sb = sb("out_sb", [P, TILES, P])

        bank_a, bank_b, bank_c, bank_d = bank("bank_a"), bank("bank_b"), bank("bank_c"), bank("bank_d")
        hid_ps = [bank("hid_ps0"), bank("hid_ps1")]
        comb_ps = bank("comb_ps")
        y_ps = bank("y_ps")

        s_const = sem("s_const")
        s_cvec = sem("s_cvec")
        s_tokw = sem("s_tokw")
        s_weights = sem("s_weights")
        s_exp0 = sem("s_exp0")
        s_wt_ps = sem("s_wt_ps")
        s_ident = sem("s_ident")
        s_x = [sem(f"s_xin{j}") for j in range(QUAD)]
        s_tok_hi = sem("s_tok_hi")
        s_tok_lo = sem("s_tok_lo")
        s_xpad = sem("s_xpad")
        s_gate_w = sem("s_gate_w")
        s_decay = sem("s_decay")
        s_powers = sem("s_powers")
        s_xT = sem("s_xT")
        s_xhi = sem("s_xhi")
        s_xlo = sem("s_xlo")
        s_conv = sem("s_conv")
        s_relu = sem("s_relu")
        s_stat = sem("s_stat")
        s_bn = sem("s_bn")
        s_bnp = sem("s_bnp")
        names = ("hfm hT st1 rstd1 xn res xnT xnhi xnlo q k v qneg kneg qexp kexp qpos kpos qdec kdec qone qone2 vfm ksum "
                 "qks kT vT ktm vpar mem_ps mem sc_ps sc num numsb den_ps den rden numT attntm attnT attn "
                 "proj_ps proj st2 rstd2 projg res2 st3 rstd3 x3 x3T x3fm x3hi x3lo gate_ps top topat istop "
                 "shifted expd expsum pickden pickrec route combine combT combfm ydone l1 hid cb mix mixhi mixlo mixlo2 l2 yfm yT "
                 "outsb store").split()
        S = {n: sem("s_" + n) for n in names}

        block = ctx.enter_context(nc.Block())

        def split3(pe, dst, w_hi, w_lo, m_hi, m_lo, start, stop):
            pe.matmul(dst, w_hi, m_hi, start=start, stop=False)
            pe.matmul(dst, w_lo, m_hi, start=False, stop=False)
            return pe.matmul(dst, w_hi, m_lo, start=False, stop=stop)

        def quads(eng, body):
            body(0, True, False)
            with eng.Fori(1, B // QUAD - 1) as quad:
                body(quad, False, False)
            body(B // QUAD - 1, False, True)

        def skewed(eng, step):
            step(-1, True, False, False, False)
            step(0, True, True, False, False)
            step(1, True, True, True, False)
            step(2, True, True, True, True)
            with eng.Fori(3, B - 1) as i:
                step(i, True, True, True, True)
            step(B - 1, False, True, True, True)
            step(B, False, False, True, True)
            step(B + 1, False, False, False, True)

        def wait_lower(eng, b, e):
            mine, name = (LOWER_POOL, "mixlo") if e in LOWER_POOL else (LOWER_DVE, "mixlo2")
            eng.wait_ge(S[name], len(mine) * b + mine.index(e) + 1)

        def lower(eng, b, e):
            eng.wait_ge(S["mixhi"], UNITS * b + e + 1)
            eng.tensor_tensor(mixed_lo[:, e % 4], mixed[:, e % 3], mixed_hi[:, e % 4].bitcast(F32), ALU.subtract
                              ).then_inc(S["mixlo" if e in LOWER_POOL else "mixlo2"], 1)

        def diagonal(t, c, n):
            v = t[:, c:c + n]
            return bass.AP(v.tensor, v.offset, [list(v.ap[0]), [4 * HD, n], [3 * HD, 2], [1, HD]])

        def by_tiles(cols):
            return cols.rearrange("p (c n) -> p c n", n=P)

        def over_tiles(row):
            return row.unsqueeze(1).to_broadcast([P, TILES, row.shape[1]])

        def over_cols(cols, n):
            return cols.unsqueeze(2).to_broadcast([P, TILES, n])

        @block.sync
        def _(sp):
            def load_x(b, j):
                sp.dma_start(x_in[0:XROWS, j], x[b].rearrange("(c p) f -> p c f", p=XROWS)).then_inc(s_x[j], 16)

            sp.dma_start(tok_w_raw[:, :, :], tok_w.rearrange("o (i f) -> o i f", i=TAPS)).then_inc(s_tokw, 16)
            for j in range(QUAD):
                load_x(j, j)
            loads = [
                (tok_vec[:, 0:1], tok_b.unsqueeze(1)), (tok_vec[:, 1:2], tok_gamma.unsqueeze(1)),
                (tok_vec[:, 2:3], tok_beta.unsqueeze(1)),
                (logits_in[:, :], bass.AP(decay_logits.tensor, 0, [[1, HEADS], [0, HD], [1, 1]])),
                (gate_raw[:, :], gate_w), (wout_sb[:, :], wout),
                (qkv_raw[:, :, :], wqkv.rearrange("d (j n) -> d j n", j=3)),
                (qkv_bias[:, :], bqkv.rearrange("(j p) -> p j", j=3)),
                (l1_raw[:, 0:EXPERTS, :], w1.rearrange("e h f -> h e f")), (l1_raw[:, EXPERTS, :], sw1),
                (l2_raw[:, 0:EXPERTS, :], w2.rearrange("e f h -> f e h")), (l2_raw[:, EXPERTS, :], sw2),
                (l1_bias[:, 0:EXPERTS], b1.rearrange("e f -> f e")), (l1_bias[:, EXPERTS:UNITS], sb1.unsqueeze(1)),
                (l2_bias[:, :], sb2.unsqueeze(1)),
                (bout_row[:, :], bout.partition_broadcast(P)), (gamma_row[:, :], ln_gamma.partition_broadcast(P)),
                (beta_row[:, :], ln_beta.partition_broadcast(P)),
            ] + [(b2_raw[EXPERTS * n:EXPERTS * (n + 1), :], b2) for n in range(PARTS)]
            assert len(loads) == WEIGHT_LOADS
            for dst, src in loads:
                sp.dma_start(dst, src, allow_slow_non_contiguous=True).then_inc(s_weights, 16)
            with sp.Fori(1, B // QUAD) as quad:
                for j in range(QUAD):
                    sp.wait_ge(s_xT, QUAD * quad + j - (QUAD - 1))
                    load_x(QUAD * quad + j, j)
            with sp.Fori(0, B) as b:
                sp.wait_ge(S["outsb"], b + 1)
                sp.dma_start(out[b, 0:(TILES - 1) * P].rearrange("(c p) f -> p c f", p=P),
                             out_sb[:, 0:TILES - 1]).then_inc(S["store"], 16)
                sp.dma_start(out[b, (TILES - 1) * P:T], out_sb[0:LAST, TILES - 1]).then_inc(S["store"], 16)
            sp.wait_ge(S["store"], 32 * B)

        @block.gpsimd
        def _(pool):
            count = 0

            def made(ins):
                nonlocal count
                count += 1
                ins.then_inc(s_const, 1)

            pool.memset(ident[:, :], 0.0).then_inc(s_ident, 1)
            pool.wait_ge(s_ident, 1)
            pool.affine_select(out=ident[:, :], in_=ident[:, :], compare_op=ALU.not_equal, fill=1.0,
                               base=0, pattern=[[-1, P]], channel_multiplier=1).then_inc(s_ident, 1)
            pool.memset(x_hi[:, :, T_IN:XW].bitcast(F32), 0.0).then_inc(s_xpad, 1)
            pool.memset(x_lo[:, :, T_IN:XW].bitcast(F32), 0.0).then_inc(s_xpad, 1)
            made(pool.memset(causal[:, :], 1.0))
            made(pool.memset(head_block[:, :], 1.0))
            made(pool.memset(ones[:, :], 1.0))
            made(pool.memset(minus_half[:, :], -0.5))
            made(pool.memset(part_select[:, :, :], 0.0))
            made(pool.memset(head_sum[:, :], 0.0))
            made(pool.memset(tiny[:, :], 1e-20))
            made(pool.memset(zeros[:, :], 0.0))
            made(pool.memset(gate[:, :], 0.0))
            made(pool.memset(eps_sb[:, :], EPS))
            for e in range(EXPERTS):
                made(pool.memset(expert_ids[:, e:e + 1], float(e)))
            for t in (h_fm[:, T:TP], q_dec[:, TE:TP], k_dec[:, TE:TP], q_one[:, :, TE:TP], v_fm[:, TE:TP],
                      q_ksum[:, TE:TP], y_fm[:, TE:TP], v_par[:, :, :, :]):
                made(pool.memset(t, 0.0))
            pool.wait_ge(s_const, count)
            made(pool.affine_select(out=causal[:, :], in_=causal[:, :], compare_op=ALU.is_ge, fill=0.0,
                                    base=0, pattern=[[1, P]], channel_multiplier=-1))
            hb = head_block[:, :].rearrange("p (h e) -> p h e", h=HEADS)
            made(pool.affine_select(out=hb, in_=hb, compare_op=ALU.is_ge, fill=0.0,
                                    base=0, pattern=[[-HD, HEADS], [0, HD]], channel_multiplier=1))
            pool.wait_ge(s_const, count)
            made(pool.affine_select(out=hb, in_=hb, compare_op=ALU.is_ge, fill=0.0,
                                    base=HD - 1, pattern=[[HD, HEADS], [0, HD]], channel_multiplier=-1))
            for part in range(PARTS):
                made(pool.affine_select(out=part_select[:, :, :], in_=part_select[:, :, :],
                                        compare_op=ALU.not_equal, fill=1.0, base=-EXPERTS * part,
                                        pattern=[[-1, EXPERTS], [0, P]], channel_multiplier=1))
                pool.wait_ge(s_const, count)
            assert count == CONSTS

            steps = 0
            pool.wait_ge(s_decay, 4)
            pool.tensor_copy(powers[:, :, 0:1], ones[:, 0:2].unsqueeze(2)).then_inc(s_powers, 1)
            for n in range(9):
                w = 1 << n
                steps += 1
                pool.wait_ge(s_powers, steps)
                if n:
                    pool.tensor_tensor(decay[:, :, n], decay[:, :, n - 1], decay[:, :, n - 1], ALU.mult
                                       ).then_inc(s_powers, 1)
                    steps += 1
                    pool.wait_ge(s_powers, steps)
                pool.tensor_tensor(powers[:, :, w:2 * w], powers[:, :, 0:w],
                                   decay[:, :, n:n + 1].to_broadcast([P, 2, w]), ALU.mult).then_inc(s_powers, 1)
            assert steps + 1 == POWERS

            pool.wait_ge(s_bn, 1)
            pool.tensor_tensor(tok_var[:, :], tok_mv[:, 1:2], eps_sb[:, 0:1], ALU.add).then_inc(s_bnp, 1)
            pool.wait_ge(s_bnp, 1)
            pool.tensor_tensor(tok_rstd[:, :], tok_var[:, :], minus_half[:, 0:1], ALU.pow).then_inc(s_bnp, 1)

            def rstd(n, b, stats, name):
                done = S[name]
                pool.wait_ge(stats, 2 * TILES * b + 2 * TILES)
                pool.tensor_tensor(ln_var[:, n], ln_mv[:, n, :, 1], eps_sb[:, :], ALU.add).then_inc(done, 1)
                pool.wait_ge(done, NORM * b + 1)
                pool.tensor_tensor(ln_rstd[:, n], ln_var[:, n], minus_half[:, :], ALU.pow).then_inc(done, 1)
                pool.tensor_tensor(ln_nmean[:, n], zeros[:, :], ln_mv[:, n, :, 0], ALU.subtract).then_inc(done, 1)
                pool.wait_ge(done, NORM * b + 3)
                pool.tensor_tensor(ln_shift[:, n], ln_nmean[:, n], ln_rstd[:, n], ALU.mult).then_inc(done, 1)

            def step(i, s0, s1, s2, s3):
                b = i - 1

                def lower_half(e):
                    if s3:
                        lower(pool, i - 2, e)

                lower_half(0)
                lower_half(1)
                lower_half(2)
                if s2:
                    rstd(1, b, S["st2"], "rstd2")
                lower_half(4)
                if s2:
                    rstd(2, b, S["st3"], "rstd3")
                if s1:
                    pool.wait_ge(S["qdec"], i + 1)
                    pool.wait_ge(S["ksum"], i + 1)
                    pool.wait_ge(S["den_ps"], i)
                    pool.tensor_tensor(q_ksum[:, 0:TE], q_dec[:, 0:TE], k_sum[:, :], ALU.mult).then_inc(S["qks"], 1)
                lower_half(6)
                if s0:
                    rstd(0, i + 1, S["st1"], "rstd1")
                if s2:
                    route(b)

            def route(b):
                n = 0

                def then(ins, wait=True):
                    nonlocal n
                    n += 1
                    ins.then_inc(S["route"], 1)
                    if wait:
                        pool.wait_ge(S["route"], ROUTE * b + n)

                pool.wait_ge(S["top"], TILES * b + TILES)
                pool.wait_ge(S["expd"], b)
                pool.tensor_tensor(shifted[:, :, :], top8[:, :, :], over_cols(top8[:, :, 0], EXPERTS),
                                   ALU.subtract).then_inc(S["shifted"], 1)
                pool.wait_ge(S["expd"], b + 1)
                then(pool.tensor_tensor(pick_sum[:, :], expd[:, :, 0], expd[:, :, 1], ALU.add), wait=False)
                pool.wait_ge(S["expsum"], b + 1)
                then(pool.tensor_tensor(exp_tiny[:, :], exp_sum[:, :], tiny[:, :], ALU.mult))
                pool.wait_ge(S["pickrec"], b)
                pool.tensor_tensor(pick_den[:, :], exp_tiny[:, :], pick_sum[:, :], ALU.add).then_inc(S["pickden"], 1)
                pool.wait_ge(S["pickrec"], b + 1)
                then(pool.tensor_tensor(top_w[:, :, :], expd[:, :, 0:2], over_cols(pick_rec[:, :], 2), ALU.mult))
                pool.wait_ge(S["istop"], b + 1)
                then(pool.tensor_tensor(placed[:, :, :, :], is_top[:, :, :, :],
                                        top_w[:, :, :].unsqueeze(3).to_broadcast([P, TILES, 2, EXPERTS]), ALU.mult))
                pool.wait_ge(S["combT"], b)
                then(pool.tensor_tensor(comb_parts[:, :, 0], placed[:, :, 0], placed[:, :, 1], ALU.add), wait=False)
                then(pool.tensor_tensor(combine[:, :, :], placed[:, :, 0], placed[:, :, 1], ALU.add))
                then(pool.tensor_tensor(comb_parts[:, :, 1], combine[:, :, :], comb_parts[:, :, 0], ALU.subtract),
                     wait=False)
                then(pool.tensor_tensor(comb_rest[:, :, :], combine[:, :, :], comb_parts[:, :, 0], ALU.subtract))
                assert n == ROUTE
                pool.tensor_tensor(comb_parts[:, :, 2], comb_rest[:, :, :], comb_parts[:, :, 1], ALU.subtract
                                   ).then_inc(S["combine"], 1)

            skewed(pool, step)

        @block.scalar
        def _(act):
            def x_upper(quad, j, first):
                b = QUAD * quad + j
                act.wait_ge(s_xT, b + 1)
                if not first:
                    act.wait_ge(s_conv, b - 1)
                act.activation(x_hi[:, j % 2, 0:T_IN], (bank_a, bank_b)[j % 2][:, 0:T_IN], ACT.Copy
                               ).then_inc(s_xhi, 1)

            def relu_tok(quad, j):
                b = QUAD * quad + j
                act.wait_ge(s_conv, b + 1)
                act.activation(seqs[:, b, 0:T], (bank_c, bank_d)[j % 2][:, 0:T], ACT.Relu, bias=tok_vec[:, 0:1]
                               ).then_inc(s_relu, 1)

            def turn(quad, first, last):
                if last:
                    act.activation(decay[:, 1, 0:1], logits_in[:, :], ACT.Exp, scale=-1.0).then_inc(s_exp0, 1)
                for j in range(QUAD):
                    if j + 1 < QUAD:
                        x_upper(quad, j + 1, first and j == 0)
                    elif not last:
                        x_upper(quad + 1, 0, False)
                    if first and j == 0:
                        act.wait_ge(s_weights, 16 * WEIGHT_LOADS)
                    relu_tok(quad, j)

            x_upper(0, 0, True)
            act.wait_ge(s_wt_ps, TAPS)
            act.activation(tok_hi[:, 0:4], bank_c[:, :].rearrange("p (i n) -> p i n", n=P), ACT.Copy
                           ).then_inc(s_tok_hi, 1)
            act.activation(tok_hi[:, 4], bank_d[:, 0:P], ACT.Copy).then_inc(s_tok_hi, 1)
            quads(act, turn)

            def step(i, s0, s1, s2, s3):
                b2_, b3 = i - 1, i - 2

                def relu(e):
                    if not s3:
                        return
                    act.wait_ge(S["l1"], UNITS * b3 + e + 1)
                    if e < EXPERTS:
                        act.wait_ge(S["mix"], EXPERTS * b3 + max(e - 2, 0))
                        dst = hid[:, e % 3]
                    else:
                        wait_lower(act, b3, e - 3)
                        dst = mixed[:, e % 3]
                    act.activation(dst, hid_ps[e % 2][:, 0:TE], ACT.Relu, bias=l1_bias[:, e:e + 1]
                                   ).then_inc(S["hid"], 1)

                def mix_upper(e):
                    if not s3:
                        return
                    act.wait_ge(S["l2"], UNITS * b3 + max(e - 3, 0))
                    if e < EXPERTS:
                        act.wait_ge(S["mix"], EXPERTS * b3 + e + 1)
                    else:
                        act.wait_ge(S["hid"], UNITS * b3 + UNITS)
                    act.activation(mixed_hi[:, e % 4], mixed[:, e % 3], ACT.Copy).then_inc(S["mixhi"], 1)

                def normalize(n, b, dst, src, name, stats):
                    act.wait_ge(S[stats], NORM * b + NORM)
                    for c in range(TILES):
                        act.activation(dst[:, c], src(c), ACT.Identity, bias=ln_shift[:, n, c:c + 1],
                                       scale=ln_rstd[:, n, c:c + 1]).then_inc(S[name], 1)

                relu(0)
                relu(1)
                if s2:
                    act.wait_ge(S["attnT"], b2_ + 1)
                    act.wait_ge(S["proj_ps"], b2_)
                    act.activation(attn[:, :], bank_b[:, 0:TP], ACT.Copy).then_inc(S["attn"], 1)
                if s1:
                    act.wait_ge(S["xnT"], i + 1)
                    act.wait_ge(S["v"], i)
                    act.activation(xn_hi[:, :], bank_c[:, 0:TE], ACT.Copy).then_inc(S["xnhi"], 1)
                relu(2)
                mix_upper(0)
                relu(3)
                if s1:
                    act.wait_ge(S["k"], i + 1)
                    act.activation(k_neg[:, :], bank_b[:, 0:TE], ACT.Relu, bias=qk_nbias[:, 1:2], scale=-1.0
                                   ).then_inc(S["kneg"], 1)
                    act.wait_ge(S["kneg"], i + 1)
                    act.wait_ge(S["kpos"], i)
                    act.activation(k_exp[:, :], k_neg[:, :], ACT.Exp, scale=-1.0).then_inc(S["kexp"], 1)
                mix_upper(1)
                relu(4)
                if s1:
                    act.wait_ge(S["q"], i + 1)
                    act.activation(q_neg[:, :], bank_a[:, 0:TE], ACT.Relu, bias=qk_nbias[:, 0:1], scale=-1.0
                                   ).then_inc(S["qneg"], 1)
                    act.wait_ge(S["qneg"], i + 1)
                    act.wait_ge(S["qpos"], i)
                    act.activation(q_exp[:, :], q_neg[:, :], ACT.Exp, scale=-1.0).then_inc(S["qexp"], 1)
                relu(5)
                if s1:
                    act.wait_ge(S["v"], i + 1)
                    act.wait_ge(S["vT"], i)
                    act.activation(v_fm[:, 0:TE], bank_c[:, 0:TE], ACT.Identity, bias=qkv_bias[:, 2:3]
                                   ).then_inc(S["vfm"], 1)
                mix_upper(2)
                mix_upper(3)
                if s1:
                    act.wait_ge(S["vT"], i + 1)
                    act.wait_ge(S["num"], TILES * i)
                    act.activation(diagonal(v_par, 0, TILES * PAIRS),
                                   bank_c[:, 0:TP].rearrange("p (g a f) -> p g a f", a=2, f=HD), ACT.Copy
                                   ).then_inc(S["vpar"], 1)
                    act.wait_ge(S["kT"], i + 1)
                    act.wait_ge(S["mem_ps"], i)
                    act.activation(k_tm[:, :, :], bank_d[:, 0:(TILES - 1) * P].rearrange("p (c n) -> p c n", n=P),
                                   ACT.Copy).then_inc(S["ktm"], 1)
                if s1:
                    act.wait_ge(S["qdec"], i + 1)
                    act.wait_ge(S["sc_ps"], 2 * TILES * i)
                    for m in (0, 1):
                        act.activation(q_one[:, m, 0:TE], q_dec[:, 0:TE], ACT.Copy, scale=head_mod[:, m:m + 1]
                                       ).then_inc(S["qone"], 1)
                relu(6)
                mix_upper(4)
                relu(7)
                mix_upper(5)
                mix_upper(6)
                mix_upper(7)
                relu(8)
                if s2:
                    act.wait_ge(S["x3T"], b2_)
                    normalize(2, b2_, x3_tm, lambda c: seqs[:, b2_, c * P:(c + 1) * P], "x3", "rstd3")
                mix_upper(8)
                if s2:
                    act.wait_ge(S["x3T"], b2_ + 1)
                    act.wait_ge(S["x3lo"], b2_)
                    act.activation(x3_fm[:, :], bank_b[:, 0:TP], ACT.Copy).then_inc(S["x3fm"], 1)
                    act.activation(x3_hi[:, :], bank_b[:, 0:TE], ACT.Copy).then_inc(S["x3hi"], 1)
                if s2:
                    act.wait_ge(S["shifted"], b2_ + 1)
                    act.wait_ge(S["route"], ROUTE * b2_)
                    act.activation(expd[:, :, :], shifted[:, :, :], ACT.Exp).then_inc(S["expd"], 1)
                if s3:
                    act.wait_ge(S["ydone"], b3 + 1)
                    act.wait_ge(S["yT"], b3)
                    act.activation(y_fm[:, 0:TE], y_ps[:, 0:TE], ACT.Identity, bias=l2_bias[:, 0:1]
                                   ).then_inc(S["yfm"], 1)
                if s1:
                    act.wait_ge(S["num"], TILES * i + TILES)
                    act.wait_ge(S["numT"], i)
                    act.activation(num_sb[:, :], bank_d[:, 0:TP], ACT.Copy).then_inc(S["numsb"], 1)
                if s0:
                    act.wait_ge(S["xnT"], i + 1)
                    normalize(0, i + 1, xn_tm, lambda c: bank_a[:, c * P:(c + 1) * P], "xn", "rstd1")

            skewed(act, step)

        @block.tensor
        def _(pe):
            def transpose_x(quad, j, first):
                pe.wait_ge(s_x[j], 16 * quad + 16)
                if not first:
                    pe.wait_ge(s_xlo, QUAD * quad + j - 1)
                for c in range(TILES):
                    ins = pe.transpose((bank_a, bank_b)[j % 2][:, c * XROWS:(c + 1) * XROWS], x_in[0:XROWS, j, c],
                                       ident[0:XROWS, 0:XROWS])
                ins.then_inc(s_xT, 1)

            def conv(quad, j, first):
                b = QUAD * quad + j
                pe.wait_ge(s_xlo, b + 1)
                if not first:
                    pe.wait_ge(s_relu, b - 1)
                for i in range(TAPS):
                    ins = split3(pe, (bank_c, bank_d)[j % 2][:, 0:TE], tok_hi[:, i], tok_lo[:, i],
                                 x_hi[:, j % 2, i:i + TE], x_lo[:, j % 2, i:i + TE], i == 0, i == TAPS - 1)
                ins.then_inc(s_conv, 1)

            def turn(quad, first, last):
                for j in range(QUAD):
                    if j + 1 < QUAD:
                        transpose_x(quad, j + 1, first and j == 0)
                    elif not last:
                        transpose_x(quad + 1, 0, False)
                    if first and j == 0:
                        pe.wait_ge(s_xpad, 2)
                        pe.wait_ge(s_tok_lo, 2)
                    conv(quad, j, first and j < 2)

            pe.wait_ge(s_ident, 2)
            pe.wait_ge(s_tokw, 16)
            for i in range(TAPS):
                dst = bank_c[:, i * P:(i + 1) * P] if i < 4 else bank_d[:, 0:P]
                ins = pe.transpose(dst, tok_w_raw[:, i], ident[:, :])
                ins.then_inc(s_wt_ps, 1)
            transpose_x(0, 0, True)
            quads(pe, turn)

            pe.wait_ge(s_weights, 16 * WEIGHT_LOADS)
            pe.transpose(hid_ps[0][:, 0:EXPERTS], gate_raw[:, :], ident[0:EXPERTS, 0:EXPERTS]).then_inc(s_gate_w, 1)
            pe.wait_ge(s_const, CONSTS)
            pe.wait_ge(s_stat, B)
            pe.wait_ge(s_cvec, CVEC_ALL)

            def tile(t, c):
                return t[:, c * P:(c + 1) * P]

            def step(i, s0, s1, s2, s3):
                b2_, b3 = i - 1, i - 2
                fixed = isinstance(i, int)

                def first(e):
                    if s3 and e < UNITS:
                        pe.wait_ge(S["hid"], UNITS * b3 + max(e - 1, 0))
                        if e == 0:
                            pe.wait_ge(S["x3lo"], b3 + 1)
                            pe.wait_ge(S["den"], min(i, B) if fixed else i)
                        if e == 1:
                            pe.wait_ge(S["topat"], TILES * (b3 + 1))
                        split3(pe, hid_ps[e % 2][:, 0:TE], l1_hi[:, e], l1_lo[:, e], x3_hi[:, :], x3_lo[:, :],
                               True, True).then_inc(S["l1"], 1)

                def weights(e):
                    if s3 and 0 <= e < EXPERTS:
                        if e == 0:
                            pe.wait_ge(S["combfm"], b3 + 1)
                        pe.wait_ge(S["mix"], EXPERTS * b3 + e)
                        pe.matmul(comb_ps[:, 0:TE], part_select[:, e], comb_fm[:, 0:TE], start=True, stop=True
                                  ).then_inc(S["cb"], 1)

                def second(e):
                    if s3 and 0 <= e < UNITS:
                        if e == 0:
                            pe.wait_ge(S["yfm"], b3)
                        wait_lower(pe, b3, e)
                        split3(pe, y_ps[:, 0:TE], l2_hi[:, e], l2_lo[:, e], mixed_hi[:, e % 4], mixed_lo[:, e % 4],
                               e == 0, False).then_inc(S["l2"], 1)
                        if e == UNITS - 1:
                            for n in range(PARTS):
                                ins = pe.matmul(y_ps[:, 0:TE], b2_parts[:, n], comb_fm[:, 0:TE], start=False,
                                                stop=(n == PARTS - 1))
                            ins.then_inc(S["ydone"], 1)

                def unit(e):
                    first(e)
                    weights(e - 1)
                    second(e - 5)

                def attend(c):
                    pe.wait_ge(S["sc"], 2 * TILES * i + 2 * c + 2)
                    dst = tile(bank_d, c)
                    if c:
                        pe.matmul(dst, memory[:, c - 1], tile(q_dec, c), start=True, stop=True)
                    for a in range(2):
                        for g in range(PAIRS):
                            rows = slice(2 * HD * g, 2 * HD * (g + 1))
                            ins = pe.matmul(bank_d[rows, c * P:(c + 1) * P], v_par[:, c * PAIRS + g, a],
                                            scores[:, c, 2 * g + a], start=(c == 0 and a == 0),
                                            stop=(c > 0 or a == 1), skip_group_check=(c > 0))
                    ins.then_inc(S["num"], 1)

                def score(c, half, dst):
                    rows = slice(64 * half, 64 * half + 64)
                    pe.matmul(dst[:, :].rearrange("p (m t) -> p m t", m=HALF), k_dec[rows, c * P:(c + 1) * P],
                              q_one[rows, :, c * P:(c + 1) * P], start=True, stop=True).then_inc(S["sc_ps"], 1)

                if s2:
                    pe.wait_ge(S["numsb"], b2_ + 1)
                    for c in range(TILES):
                        ins = pe.transpose(tile(bank_d, c), tile(num_sb, c), ident[:, :])
                    ins.then_inc(S["numT"], 1)
                first(0)
                first(1)
                if s3:
                    pe.wait_ge(S["combine"], b3 + 1)
                    comb_t = bank_c[:, :].bitcast(BF16)
                    for c in range(TILES):
                        ins = pe.transpose(comb_t[0:PARTS * EXPERTS, c * P:(c + 1) * P],
                                           comb_parts[:, c].rearrange("p n e -> p (n e)"), ident_bf[:, :])
                    ins.then_inc(S["combT"], 1)
                first(2)
                if s2:
                    pe.wait_ge(S["attntm"], b2_ + 1)
                    pe.wait_ge(S["x3hi"], b2_)
                    if not fixed or i > 2:
                        pe.wait_ge(S["outsb"], i - 2)
                    for c in range(TILES):
                        ins = pe.transpose(tile(bank_b, c), attn_tm[:, c], ident[:, :])
                    ins.then_inc(S["attnT"], 1)
                weights(0)
                if s1:
                    pe.wait_ge(S["xn"], TILES * i + TILES)
                    if s3:
                        pe.wait_ge(S["combfm"], b3 + 1)
                    for c in range(TILES):
                        ins = pe.transpose(tile(bank_c, c), xn_tm[:, c], ident[:, :])
                    ins.then_inc(S["xnT"], 1)
                first(3)
                weights(1)
                if s2:
                    pe.wait_ge(S["attn"], b2_ + 1)
                    for c in range(TILES):
                        ins = pe.matmul(tile(bank_d, c), tile(attn, c), wout_sb[:, :], start=True, stop=True)
                    ins.then_inc(S["proj_ps"], 1)
                if s1:
                    pe.wait_ge(S["xnlo"], i + 1)
                    for n, (dst, name) in ((1, (bank_b, "k")), (0, (bank_a, "q")), (2, (bank_c, "v"))):
                        if n == 0:
                            pe.wait_ge(S["res"], i + 1)
                        if n == 2:
                            weights(2)
                        split3(pe, dst[:, 0:TE], qkv_hi[:, n], qkv_lo[:, n], xn_hi[:, :], xn_lo[:, :], True, True
                               ).then_inc(S[name], 1)
                if not s1:
                    weights(2)
                first(4)
                weights(3)
                unit(5)
                unit(6)
                if s1:
                    pe.wait_ge(S["vfm"], i + 1)
                    for c in range(TILES):
                        ins = pe.transpose(tile(bank_c, c), tile(v_fm, c), ident[:, :])
                    ins.then_inc(S["vT"], 1)
                if s1:
                    pe.wait_ge(S["kdec"], i + 1)
                    if s2:
                        pe.wait_ge(S["proj"], b2_ + 1)
                    for c in range(TILES - 1):
                        ins = pe.transpose(tile(bank_d, c), tile(k_dec, c), ident[:, :])
                    ins.then_inc(S["kT"], 1)
                unit(7)
                if s1:
                    pe.wait_ge(S["ktm"], i + 1)
                    pe.wait_ge(S["vpar"], i + 1)
                    pe.wait_ge(S["qpos"], i + 1)
                    for n in range(TILES - 1):
                        for c in range(n + 1):
                            ins = pe.matmul(tile(bank_a, n), k_tm[:, c], diagonal(v_par, c * PAIRS, PAIRS),
                                            start=(c == 0), stop=(c == n))
                    ins.then_inc(S["mem_ps"], 1)
                    pe.wait_ge(S["qone"], 2 * i + 2)
                    pe.wait_ge(S["qone2"], 2 * i + 2)
                    score(0, 0, bank_b)
                    score(0, 1, bank_c)
                unit(8)
                if s1:
                    pe.wait_ge(S["mem"], i + 1)
                    score(1, 0, bank_a)
                    pe.wait_ge(S["sc"], 2 * TILES * i + 1)
                    score(1, 1, bank_b)
                    attend(0)
                unit(9)
                if s1:
                    score(2, 0, bank_c)
                    pe.wait_ge(S["sc"], 2 * TILES * i + 3)
                    score(2, 1, bank_a)
                    attend(1)
                unit(10)
                if s2:
                    pe.wait_ge(S["x3"], TILES * b2_ + TILES)
                    if s1:
                        pe.wait_ge(S["sc"], 2 * TILES * i + 4)
                    for c in range(TILES):
                        ins = pe.transpose(tile(bank_b, c), x3_tm[:, c], ident[:, :])
                    ins.then_inc(S["x3T"], 1)
                if s0:
                    pe.wait_ge(S["hfm"], i + 2)
                    if s1:
                        pe.wait_ge(S["sc"], 2 * TILES * i + 6)
                    for c in range(TILES):
                        ins = pe.transpose(tile(bank_a, c), tile(h_fm, c), ident[:, :])
                    ins.then_inc(S["hT"], 1)
                unit(11)
                if s2:
                    pe.wait_ge(S["x3fm"], b2_ + 1)
                    if s3:
                        pe.wait_ge(S["hid"], UNITS * b3 + UNITS - 1)
                    for c in range(TILES):
                        ins = pe.matmul(tile(hid_ps[1], c)[:, 0:GATE_COLS], tile(x3_fm, c), gate[:, :],
                                        start=True, stop=True)
                    ins.then_inc(S["gate_ps"], 1)
                unit(12)
                unit(13)
                if s1:
                    attend(2)
                if s1:
                    pe.wait_ge(S["qks"], i + 1)
                    if s3:
                        pe.wait_ge(S["hid"], UNITS * b3 + UNITS)
                    for c in range(TILES):
                        ins = pe.matmul(tile(hid_ps[0], c)[:, 0:GATE_COLS], tile(q_ksum, c), head_sum[:, :],
                                        start=True, stop=True)
                    ins.then_inc(S["den_ps"], 1)
                if s3:
                    pe.wait_ge(S["yfm"], b3 + 1)
                    if s2:
                        pe.wait_ge(S["x3hi"], b2_ + 1)
                    else:
                        pe.wait_ge(S["outsb"], b3)
                    for c in range(TILES):
                        ins = pe.transpose(tile(bank_b, c), tile(y_fm, c), ident[:, :])
                    ins.then_inc(S["yT"], 1)

            skewed(pe, step)

        @block.vector
        def _(dve):
            done = 0

            def link(ins):
                nonlocal done
                done += 1
                ins.then_inc(s_cvec, 1)
                dve.wait_ge(s_cvec, done)

            def halves(hi, lo, src):
                link(dve.tensor_copy(hi, src))
                link(dve.tensor_tensor(lo, src, hi.bitcast(F32), ALU.subtract))

            dve.wait_ge(s_tok_hi, 1)
            dve.tensor_tensor(tok_lo[:, 0:4], bank_c[:, :].rearrange("p (i n) -> p i n", n=P),
                              tok_hi[:, 0:4].bitcast(F32), ALU.subtract).then_inc(s_tok_lo, 1)
            dve.wait_ge(s_tok_hi, 2)
            dve.tensor_tensor(tok_lo[:, 4], bank_d[:, 0:P], tok_hi[:, 4].bitcast(F32), ALU.subtract
                              ).then_inc(s_tok_lo, 1)

            def x_lower(quad, j):
                dve.wait_ge(s_xhi, QUAD * quad + j + 1)
                dve.tensor_tensor(x_lo[:, j % 2, 0:T_IN], (bank_a, bank_b)[j % 2][:, 0:T_IN],
                                  x_hi[:, j % 2, 0:T_IN].bitcast(F32), ALU.subtract).then_inc(s_xlo, 1)

            def stats_tok(b):
                dve.wait_ge(s_relu, b + 1)
                dve.bn_stats(tok_stats[:, b], seqs[:, b, 0:T]).then_inc(s_stat, 1)

            def turn(quad, first, last):
                for j in range(QUAD):
                    if last and j == 0:
                        invert_decay()
                    if j + 1 < QUAD:
                        x_lower(quad, j + 1)
                    elif not last:
                        x_lower(quad + 1, 0)
                    if last and j == 0:
                        split_weights(l1_hi, l1_lo, l1_raw)
                    elif last and j == 1:
                        split_weights(l2_hi, l2_lo, l2_raw)
                    elif last and j == 2:
                        prepare()
                    stats_tok(QUAD * quad + j)

            def invert_decay():
                dve.wait_ge(s_exp0, 1)
                dve.tensor_scalar(decay[:, 1, 0:1], decay[:, 1, 0:1], 1.0, None, ALU.add).then_inc(s_decay, 1)
                dve.wait_ge(s_decay, 1)
                dve.reciprocal(decay[:, 0, 0:1], decay[:, 1, 0:1]).then_inc(s_decay, 3)

            def split_weights(hi, lo, src):
                dve.wait_ge(s_weights, 16 * WEIGHT_LOADS)
                halves(hi[:, :, :], lo[:, :, :], src)

            def prepare():
                dve.wait_ge(s_weights, 16 * WEIGHT_LOADS)
                dve.wait_ge(s_const, CONSTS)
                halves(qkv_hi[:, :, :], qkv_lo[:, :, :], qkv_raw)
                link(dve.tensor_scalar(qk_bias1[:, :], qkv_bias[:, 0:2], 1.0, None, ALU.add))
                link(dve.tensor_scalar(qk_nbias[:, :], qkv_bias[:, 0:2], -1.0, None, ALU.mult))
                link(dve.tensor_copy(ident_bf[:, :], ident[:, :]))
                hm = head_block[:, :].rearrange("p (h e) -> p h e", h=HEADS)
                link(dve.tensor_tensor(head_mod[:, :], hm[:, 0:HALF, 0], hm[:, HALF:HEADS, 0], ALU.add))
                link(dve.tensor_copy(head_sum[:, 0:HEADS], hm[:, :, 0]))
                link(dve.tensor_copy(b2_parts[:, 0], b2_raw[:, :]))
                link(dve.tensor_tensor(b2_rest[:, 0], b2_raw[:, :], b2_parts[:, 0], ALU.subtract))
                link(dve.tensor_copy(b2_parts[:, 1], b2_rest[:, 0]))
                link(dve.tensor_tensor(b2_rest[:, 1], b2_rest[:, 0], b2_parts[:, 1], ALU.subtract))
                link(dve.tensor_copy(b2_parts[:, 2], b2_rest[:, 1]))

            x_lower(0, 0)
            quads(dve, turn)

            dve.wait_ge(s_gate_w, 1)
            link(dve.tensor_copy(gate[:, 0:EXPERTS], hid_ps[0][:, 0:EXPERTS]))
            dve.wait_ge(s_powers, POWERS)
            dve.wait_ge(s_stat, B)
            dve.bn_aggr(tok_mv[:, :], tok_stats[:, :, :].rearrange("p b s -> p (b s)")).then_inc(s_bn, 1)
            dve.wait_ge(s_bnp, 2)
            link(dve.tensor_tensor(bn_scale[:, :], tok_vec[:, 1:2], tok_rstd[:, :], ALU.mult))
            link(dve.tensor_scalar(bn_shift[:, :], tok_mv[:, 0:1], bn_scale[:, 0:1], tok_vec[:, 2:3],
                                   ALU.mult, ALU.subtract))
            assert done == CVEC_ALL

            def token_stats(n, src, name):
                for c in range(TILES):
                    dve.bn_stats(ln_stats[:, n, c], src(c)).then_inc(S[name], 1)

            def gather_stats(n, b, name):
                dve.wait_ge(S[name], 2 * TILES * b + TILES)
                dve.memset(fence[:, n:n + 1], 0.0)
                for c in range(TILES):
                    dve.bn_aggr(ln_mv[:, n, c], ln_stats[:, n, c]).then_inc(S[name], 1)

            def step(i, s0, s1, s2, s3):
                b2_, b3 = i - 1, i - 2
                fixed = isinstance(i, int)

                def tile_a(c):
                    return bank_a[:, c * P:(c + 1) * P]

                def mix(e):
                    if not s3:
                        return
                    dve.wait_ge(S["hid"], UNITS * b3 + e + 1)
                    if e >= 3:
                        wait_lower(dve, b3, e - 3)
                    dve.wait_ge(S["cb"], EXPERTS * b3 + e + 1)
                    dve.tensor_tensor(mixed[:, e % 3], hid[:, e % 3], comb_ps[:, 0:TE], ALU.mult
                                      ).then_inc(S["mix"], 1)

                def lower_half(e):
                    if s3:
                        lower(dve, b3, e)

                def take_scores(c, n, src):
                    dve.wait_ge(S["sc_ps"], 2 * TILES * i + 2 * c + n + 1)
                    dve.tensor_tensor(scores[:, c, HALF * n:HALF * (n + 1)],
                                      src[:, :].rearrange("p (m t) -> p m t", m=HALF),
                                      causal[:, :].unsqueeze(1).to_broadcast([P, HALF, P]), ALU.mult
                                      ).then_inc(S["sc"], 1)

                if s2:
                    dve.wait_ge(S["attnT"], b2_)
                    dve.wait_ge(S["rden"], b2_ + 1)
                    dve.wait_ge(S["numT"], b2_ + 1)
                    dve.tensor_tensor(attn_tm[:, :, :].rearrange("p c (h e) -> p c h e", h=HEADS),
                                      bank_d[:, 0:TP].rearrange("p (c h e) -> p c h e", c=TILES, h=HEADS),
                                      rden[:, :, :].unsqueeze(3).to_broadcast([P, TILES, HEADS, HD]), ALU.mult
                                      ).then_inc(S["attntm"], 1)
                if s3:
                    dve.wait_ge(S["ydone"], b3)
                    dve.wait_ge(S["combT"], b3 + 1)
                    dve.tensor_copy(comb_fm[:, :], bank_c[:, :].bitcast(BF16)[0:PARTS * EXPERTS, 0:TP]
                                    ).then_inc(S["combfm"], 1)
                mix(0)
                if s1:
                    dve.wait_ge(S["xnhi"], i + 1)
                    dve.tensor_tensor(xn_lo[:, :], bank_c[:, 0:TE], xn_hi[:, :].bitcast(F32), ALU.subtract
                                      ).then_inc(S["xnlo"], 1)
                mix(1)
                if s1:
                    dve.wait_ge(S["xn"], TILES * i + TILES)
                    dve.tensor_tensor(by_tiles(seqs[:, i]), bank_a[:, 0:TP].rearrange("p (c n) -> p c n", n=P),
                                      over_tiles(beta_row[:, :]), ALU.add).then_inc(S["res"], 1)
                mix(2)
                if s2:
                    dve.wait_ge(S["proj_ps"], b2_ + 1)
                    dve.tensor_tensor(proj[:, :, :], bank_d[:, 0:TP].rearrange("p (c n) -> p c n", n=P),
                                      over_tiles(bout_row[:, :]), ALU.add).then_inc(S["proj"], 1)
                mix(3)
                if s2:
                    dve.wait_ge(S["proj"], b2_ + 1)
                    token_stats(1, lambda c: proj[:, c], "st2")
                if s1:
                    dve.wait_ge(S["kexp"], i + 1)
                    dve.scalar_tensor_tensor(out=k_pos[:, :], in0=bank_b[:, 0:TE], scalar=qk_bias1[:, 1:2],
                                             in1=k_exp[:, :], op0=ALU.add, op1=ALU.max).then_inc(S["kpos"], 1)
                mix(4)
                if s2:
                    gather_stats(1, b2_, "st2")
                if s1:
                    dve.wait_ge(S["kpos"], i + 1)
                    dve.wait_ge(S["num"], TILES * i)
                    dve.tensor_tensor(k_dec[:, 0:TE], k_pos[:, :], powers[:, 1, 0:TE], ALU.mult
                                      ).then_inc(S["kdec"], 1)
                    dve.wait_ge(S["qexp"], i + 1)
                    dve.scalar_tensor_tensor(out=q_pos[:, :], in0=bank_a[:, 0:TE], scalar=qk_bias1[:, 0:1],
                                             in1=q_exp[:, :], op0=ALU.add, op1=ALU.max).then_inc(S["qpos"], 1)
                    dve.wait_ge(S["qpos"], i + 1)
                    dve.wait_ge(S["qks"], i)
                    dve.tensor_tensor(q_dec[:, 0:TE], q_pos[:, :], powers[:, 0, 0:TE], ALU.mult
                                      ).then_inc(S["qdec"], 1)
                mix(5)
                if s1:
                    dve.wait_ge(S["sc_ps"], 2 * TILES * i)
                    dve.wait_ge(S["qdec"], i + 1)
                    for m in (2, 3):
                        dve.tensor_scalar(q_one[:, m, 0:TE], q_dec[:, 0:TE], head_mod[:, m:m + 1], None, ALU.mult
                                          ).then_inc(S["qone2"], 1)
                lower_half(3)
                mix(6)
                if s1:
                    dve.wait_ge(S["mem_ps"], i + 1)
                    dve.wait_ge(S["num"], TILES * i)
                    dve.tensor_tensor(memory[:, :, :], bank_a[:, 0:2 * P].rearrange("p (n m) -> p n m", n=2),
                                      head_block[:, :].unsqueeze(1).to_broadcast([P, 2, P]), ALU.mult
                                      ).then_inc(S["mem"], 1)
                if s2:
                    dve.wait_ge(S["st2"], 2 * TILES * b2_ + 2 * TILES)
                    for c in range(TILES):
                        dve.scalar_tensor_tensor(out=proj_g[:, c], in0=proj[:, c], scalar=ln_mv[:, 1, c, 0:1],
                                                 in1=gamma_row[:, :], op0=ALU.subtract, op1=ALU.mult
                                                 ).then_inc(S["projg"], 1)
                if s1:
                    take_scores(0, 0, bank_b)
                    take_scores(0, 1, bank_c)
                mix(7)
                if s2:
                    dve.wait_ge(S["projg"], TILES * b2_ + TILES)
                    dve.wait_ge(S["rstd2"], NORM * b2_ + NORM)
                    for c in range(TILES):
                        row = seqs[:, b2_, c * P:(c + 1) * P]
                        dve.scalar_tensor_tensor(out=row, in0=proj_g[:, c], scalar=ln_rstd[:, 1, c:c + 1], in1=row,
                                                 op0=ALU.mult, op1=ALU.add).then_inc(S["res2"], 1)
                    dve.wait_ge(S["res2"], TILES * b2_ + TILES)
                    dve.memset(fence[:, 5:6], 0.0)
                    token_stats(2, lambda c: seqs[:, b2_, c * P:(c + 1) * P], "st3")
                if s1:
                    take_scores(1, 0, bank_a)
                if s2:
                    gather_stats(2, b2_, "st3")
                if s1:
                    take_scores(1, 1, bank_b)
                lower_half(5)
                if s0:
                    dve.tensor_scalar(h_fm[:, 0:T], seqs[:, i + 1, 0:T], bn_scale[:, 0:1], bn_shift[:, 0:1],
                                      ALU.mult, ALU.subtract).then_inc(S["hfm"], 1)
                if s1:
                    dve.wait_ge(S["qks"], i)
                    dve.wait_ge(S["kdec"], i + 1)
                    dve.tensor_tensor_scan(k_sum[:, :], ones[:, 0:TE], k_dec[:, 0:TE], 0.0, ALU.mult, ALU.add
                                           ).then_inc(S["ksum"], 1)
                if s1:
                    take_scores(2, 0, bank_c)
                    take_scores(2, 1, bank_a)
                lower_half(7)
                if s0:
                    dve.wait_ge(S["hT"], i + 2)
                    token_stats(0, tile_a, "st1")
                lower_half(8)
                if s0:
                    gather_stats(0, i + 1, "st1")
                if s2:
                    dve.wait_ge(S["x3hi"], b2_ + 1)
                    dve.tensor_tensor(x3_lo[:, :], x3_fm[:, 0:TE], x3_hi[:, :].bitcast(F32), ALU.subtract
                                      ).then_inc(S["x3lo"], 1)
                if s2:
                    find_top(b2_)
                if s2:
                    dve.wait_ge(S["expd"], b2_ + 1)
                    dve.wait_ge(S["route"], ROUTE * b2_)
                    dve.tensor_reduce(exp_sum[:, :], expd[:, :, :], AX_X, ALU.add).then_inc(S["expsum"], 1)
                    dve.wait_ge(S["pickden"], b2_ + 1)
                    dve.reciprocal(pick_rec[:, :], pick_den[:, :]).then_inc(S["pickrec"], 1)
                if s1:
                    dve.wait_ge(S["den_ps"], i + 1)
                    dve.wait_ge(S["rden"], i)
                    dve.tensor_scalar(den_tm[:, :, :], hid_ps[0][:, 0:TP].rearrange("p (c n) -> p c n", n=P)[:, :, 0:HEADS],
                                      DEN_EPS * HD ** 0.5, None, ALU.add).then_inc(S["den"], 1)
                    dve.wait_ge(S["den"], i + 1)
                    dve.wait_ge(S["attntm"], i)
                    dve.reciprocal(rden[:, :, :], den_tm[:, :, :]).then_inc(S["rden"], 1)
                if s3:
                    dve.wait_ge(S["store"], 32 * b3)
                    dve.wait_ge(S["yT"], b3 + 1)
                    dve.tensor_tensor(out_sb[:, :, :], bank_b[:, 0:TP].rearrange("p (c n) -> p c n", n=P),
                                      by_tiles(seqs[:, b3]), ALU.add).then_inc(S["outsb"], 1)

            def find_top(b):
                gate_out = hid_ps[1][:, 0:TP].rearrange("p (c n) -> p c n", n=P)[:, :, 0:EXPERTS]
                dve.wait_ge(S["gate_ps"], b + 1)
                dve.wait_ge(S["shifted"], b)
                dve.memset(fence[:, 3:4], 0.0)
                for c in range(TILES):
                    dve.max(top8[:, c], gate_out[:, c]).then_inc(S["top"], 1)
                dve.wait_ge(S["top"], TILES * b + TILES)
                dve.memset(fence[:, 4:5], 0.0)
                for c in range(TILES):
                    dve.max_index(top_at[:, c], top8[:, c], gate_out[:, c]).then_inc(S["topat"], 1)
                dve.wait_ge(S["topat"], TILES * b + TILES)
                dve.wait_ge(S["combine"], b)
                dve.tensor_tensor(is_top[:, :, :, :],
                                  expert_ids[:, :].unsqueeze(1).unsqueeze(1).to_broadcast([P, TILES, 2, EXPERTS]),
                                  top_at[:, :, 0:2].unsqueeze(3).to_broadcast([P, TILES, 2, EXPERTS]), ALU.is_equal
                                  ).then_inc(S["istop"], 1)

            skewed(dve, step)


CONSTS = 18 + 8 + 3 + PARTS
WEIGHT_LOADS = 18 + PARTS
CVEC_ALL = 6 + 5 + 5 + 1 + 2
POWERS = 1 + 9 + 8
LOWER_POOL = (0, 1, 2, 4, 6)
LOWER_DVE = (3, 5, 7, 8)
NORM = 4
ROUTE = 8

_INS = ["x", "L0_tok_W", "L0_tok_b", "L0_tok_gamma", "L0_tok_beta", "L0_attn_Wqkv", "L0_attn_bqkv",
        "L0_attn_Wout", "L0_attn_bout", "L0_attn_ln_gamma", "L0_attn_ln_beta", "L0_attn_decay_logits",
        "L0_ffn_gate_w", "L0_ffn_w1", "L0_ffn_b1", "L0_ffn_w2", "L0_ffn_b2", "L0_ffn_sw1", "L0_ffn_sb1",
        "L0_ffn_sw2", "L0_ffn_sb2"]


def kernel(**inputs):
    import numpy as np
    import concourse.bacc as bacc
    from concourse.bass_utils import run_bass_kernel_spmd

    nc = bacc.Bacc("TRN2", target_bir_lowering=False, num_devices=1)
    arrays, args = {}, []
    for name in _INS:
        a = np.ascontiguousarray(inputs[name])
        arrays[f"in_{name}"] = a
        args.append(nc.dram_tensor(f"in_{name}", a.shape, mybir.dt.from_np(a.dtype), kind="ExternalInput").ap())
    b, t, d = inputs["x"].shape
    args.append(nc.dram_tensor("out", (b, t - (TAPS - 1), d), F32, kind="ExternalOutput").ap())
    build(nc, *args)
    r = run_bass_kernel_spmd(nc, [arrays], core_ids=[0])
    return r.results[0]["out"]
```
